# Optimizing a Trainium2 kernel written in Bass

```python
import numpy as np
import jax
import jax.numpy as jnp

def _softmax(x, axis=-1):
    return jax.nn.softmax(x, axis=axis)

def _gelu(x):
    return jax.nn.gelu(x, approximate=True)

def _silu(x):
    return jax.nn.silu(x)

def _sigmoid(x):
    return jax.nn.sigmoid(x)

def _layernorm(x, axis=-1, eps=1e-05):
    m = jnp.mean(x, axis=axis, keepdims=True)
    v = jnp.var(x, axis=axis, keepdims=True)
    return (x - m) / jnp.sqrt(v + eps)

def _scatter_add(tgt, idx, src, axis=0):
    return tgt.at[idx].add(src)

def _segment_sum(src, seg, n):
    return jax.ops.segment_sum(src, seg, n)
kernel_name = 'mk_adj_ffn_d1_adj_r2_41131b'

def setup_inputs(seed: int=0):
    np.random.seed(seed)
    _w = jnp.asarray

    def _rec_inputs():
        import jax
        import jax.numpy as jnp
        _gk = jax.random.key(seed)
        x = -0.0005963 + 1.001 * jax.random.normal(jax.random.fold_in(_gk, 1), (1354, 256), jnp.float32)
        _w = (1.0 + jnp.arange(1354, dtype=jnp.float32)) ** (-0.5)
        _w = _w / _w.mean()
        _pij = jnp.clip(0.00295421 * _w[:, None] * _w[None, :], 0.0, 1.0)
        _a = jax.random.uniform(jax.random.fold_in(_gk, 2), (1354, 1354)) < _pij
        _af = _a.astype(jnp.float32)
        adj = _af
        return (x, adj)
    x, adj = _rec_inputs()

    def _L0_gnn_setup():
        import jax, jax.numpy as jnp
        import numpy as np
        N = 3072
        D_IN = 256
        D_OUT = 256
        DENSITY = 0.005
        key = jax.random.key(seed)
        ks = jax.random.split(key, 12)
        x = jax.random.normal(ks[0], (N, D_IN), dtype=jnp.float32)
        adj_a = (jax.random.uniform(ks[1], (N, N)) < DENSITY).astype(jnp.float32)
        adj_b = (jax.random.uniform(ks[2], (N, N)) < DENSITY).astype(jnp.float32)
        W_sa = jax.random.normal(ks[3], (D_IN, D_OUT), dtype=jnp.float32) * (1.414 / np.sqrt(D_IN + D_OUT))
        a_sa = jax.random.normal(ks[4], (1, 2 * D_OUT), dtype=jnp.float32) * (1.414 / np.sqrt(1 + 2 * D_OUT))
        stdv = 1.0 / np.sqrt(D_OUT)
        W_gcnb = jax.random.uniform(ks[5], (D_IN, D_OUT), minval=-stdv, maxval=stdv, dtype=jnp.float32)
        b_gcnb = jax.random.uniform(ks[6], (D_OUT,), minval=-stdv, maxval=stdv, dtype=jnp.float32)
        s = 1.0 / np.sqrt(2 * D_IN)
        Wa = jax.random.uniform(ks[7], (1, 2 * D_IN), minval=-s, maxval=s, dtype=jnp.float32)
        ba = jax.random.uniform(ks[8], (1,), minval=-s, maxval=s, dtype=jnp.float32)
        Wb = jax.random.uniform(ks[9], (1, 2 * D_IN), minval=-s, maxval=s, dtype=jnp.float32)
        bb = jax.random.uniform(ks[10], (1,), minval=-s, maxval=s, dtype=jnp.float32)
        return {'x': x, 'adj_a': adj_a, 'adj_b': adj_b, 'W_sa': W_sa, 'a_sa': a_sa, 'W_gcnb': W_gcnb, 'b_gcnb': b_gcnb, 'Wa': Wa, 'ba': ba, 'Wb': Wb, 'bb': bb}
    _L0_gnn_all = _L0_gnn_setup()
    _L0_gnn_in = {k: v for k, v in _L0_gnn_all.items() if k in ('W_sa', 'a_sa', 'W_gcnb', 'b_gcnb', 'Wa', 'ba', 'Wb', 'bb')}
    del _L0_gnn_all

    def _L0_ffn_setup():
        import jax, jax.numpy as jnp
        import numpy as np
        E = 16
        K = 4
        NEG = jnp.float32(-1e+20)

        def _swiglu(x, w1, w2, w3):
            a = x @ w1
            return a * jax.nn.sigmoid(a) * (x @ w2) @ w3
        key = jax.random.key(seed)
        ks = jax.random.split(key, 9)
        B, S, D, H = (32, 256, 256, 1365)
        s = 0.02
        return {'x': jax.random.normal(ks[0], (B, S, D), jnp.float32), 'gate_w': jax.random.normal(ks[1], (D, E), jnp.float32) * s, 'routing_bias': jnp.zeros((E,), jnp.float32), 'w1': jax.random.normal(ks[2], (E, D, H), jnp.float32) * s, 'w2': jax.random.normal(ks[3], (E, D, H), jnp.float32) * s, 'w3': jax.random.normal(ks[4], (E, H, D), jnp.float32) * s, 'sw1': jax.random.normal(ks[5], (D, H), jnp.float32) * s, 'sw2': jax.random.normal(ks[6], (D, H), jnp.float32) * s, 'sw3': jax.random.normal(ks[7], (H, D), jnp.float32) * s}
    _L0_ffn_all = _L0_ffn_setup()
    _L0_ffn_in = {k: v for k, v in _L0_ffn_all.items() if k in ('gate_w', 'routing_bias', 'w1', 'w2', 'w3', 'sw1', 'sw2', 'sw3')}
    del _L0_ffn_all
    return {'x': x, 'adj': adj, 'L0_gnn_W_sa': _L0_gnn_in['W_sa'], 'L0_gnn_a_sa': _L0_gnn_in['a_sa'], 'L0_gnn_W_gcnb': _L0_gnn_in['W_gcnb'], 'L0_gnn_b_gcnb': _L0_gnn_in['b_gcnb'], 'L0_gnn_Wa': _L0_gnn_in['Wa'], 'L0_gnn_ba': _L0_gnn_in['ba'], 'L0_gnn_Wb': _L0_gnn_in['Wb'], 'L0_gnn_bb': _L0_gnn_in['bb'], 'L0_ffn_gate_w': _L0_ffn_in['gate_w'], 'L0_ffn_routing_bias': _L0_ffn_in['routing_bias'], 'L0_ffn_w1': _L0_ffn_in['w1'], 'L0_ffn_w2': _L0_ffn_in['w2'], 'L0_ffn_w3': _L0_ffn_in['w3'], 'L0_ffn_sw1': _L0_ffn_in['sw1'], 'L0_ffn_sw2': _L0_ffn_in['sw2'], 'L0_ffn_sw3': _L0_ffn_in['sw3']}

def reference(x, adj, L0_gnn_W_sa, L0_gnn_a_sa, L0_gnn_W_gcnb, L0_gnn_b_gcnb, L0_gnn_Wa, L0_gnn_ba, L0_gnn_Wb, L0_gnn_bb, L0_ffn_gate_w, L0_ffn_routing_bias, L0_ffn_w1, L0_ffn_w2, L0_ffn_w3, L0_ffn_sw1, L0_ffn_sw2, L0_ffn_sw3):
    import jax
    import jax.numpy as jnp

    def _L0_gnn_ref(x, adj_a, adj_b, W_sa, a_sa, W_gcnb, b_gcnb, Wa, ba, Wb, bb):
        import jax, jax.numpy as jnp
        import numpy as np
        N = 3072
        D_IN = 256
        D_OUT = 256
        DENSITY = 0.005
        type_sum_a = adj_a @ x
        type_sum_b = adj_b @ x
        attn_a = jax.nn.sigmoid(jnp.concatenate([type_sum_a, x], axis=1) @ Wa.T + ba)
        attn_b = jax.nn.sigmoid(jnp.concatenate([type_sum_b, x], axis=1) @ Wb.T + bb)
        h = x @ W_sa
        Hd = h.shape[1]
        s_left = h @ a_sa[0, :Hd]
        s_right = h @ a_sa[0, Hd:]
        scores = s_left[:, None] + s_right[None, :]
        e = jnp.where(adj_a != 0, jnp.exp(-jax.nn.leaky_relu(scores, 0.01)), 0.0)
        attn = e / (jnp.sum(e, axis=1, keepdims=True) + 1e-05)
        x_a = attn @ h
        x_b = adj_b @ (x @ W_gcnb) + b_gcnb
        return jax.nn.sigmoid(attn_a * x_a + attn_b * x_b)

    def _L0_ffn_ref(x, gate_w, routing_bias, w1, w2, w3, sw1, sw2, sw3):
        import jax, jax.numpy as jnp
        import numpy as np
        E = 16
        K = 4
        NEG = jnp.float32(-1e+20)

        def _swiglu(x, w1, w2, w3):
            a = x @ w1
            return a * jax.nn.sigmoid(a) * (x @ w2) @ w3
        gate_out = x @ gate_w + routing_bias
        top_v, top_i = jax.lax.top_k(gate_out, K)
        chosen = jax.nn.one_hot(top_i, E, dtype=x.dtype).sum(axis=-2)
        masked = jnp.where(chosen > 0, gate_out, NEG)
        probs = jax.nn.softmax(masked, axis=-1)
        weights = probs * chosen
        out = _swiglu(x, sw1, sw2, sw3)
        for e in range(E):
            out = out + _swiglu(x, w1[e], w2[e], w3[e]) * weights[..., e:e + 1]
        return out
    x = x + _L0_gnn_ref(_layernorm(x, axis=-1), adj, adj, L0_gnn_W_sa, L0_gnn_a_sa, L0_gnn_W_gcnb, L0_gnn_b_gcnb, L0_gnn_Wa, L0_gnn_ba, L0_gnn_Wb, L0_gnn_bb)
    x = x + _L0_ffn_ref(_layernorm(x, axis=-1)[None], L0_ffn_gate_w, L0_ffn_routing_bias, L0_ffn_w1, L0_ffn_w2, L0_ffn_w3, L0_ffn_sw1, L0_ffn_sw2, L0_ffn_sw3)[0]
    return x

_drawn_inputs = setup_inputs


def setup_inputs(seed=0):
    import zlib

    import numpy as np

    out = dict(_drawn_inputs(seed))
    spreads = {'L0_ffn_routing_bias': (0.0, 0.8)}
    factors = {'L0_gnn_a_sa': 2.923,
     'L0_gnn_b_gcnb': 8.0,
     'L0_gnn_Wa': 2.737,
     'L0_ffn_gate_w': 3.772,
     'L0_ffn_w1': 3.268,
     'L0_ffn_w2': 3.222,
     'L0_ffn_w3': 3.225}
    for name, (base, spread) in spreads.items():
        noise = np.random.default_rng([zlib.crc32(name.encode()), seed]).standard_normal(out[name].shape)
        drawn = base * np.exp(spread * noise) if base else spread * noise
        out[name] = jnp.asarray(drawn.astype(out[name].dtype))
    for name, factor in factors.items():
        out[name] = (out[name] * factor).astype(out[name].dtype)
    return out
```

```python
from contextlib import ExitStack

import concourse.bass as bass
from concourse import mybir

F32 = mybir.dt.float32
F32R = mybir.dt.float32r
U32 = mybir.dt.uint32
I32 = mybir.dt.int32
ALU = mybir.AluOpType
ACT = mybir.ActivationFunctionType
AX = mybir.AxisListType

P = 128
EPS = 1e-5
ATTN_EPS = 1e-5
TOPK = 4


def cdiv(a, b):
    return -(-a // b)


def graph_attention_and_routed_experts(nc, x, adjT, w_sa, w_saT, w_gcn, a_cols, attn_cols,
                                       attn_bias, gcn_bias, gate_w, routing_bias, w_ffn, out):
    NTOK, D = out.shape
    NT = x.shape[0] // P
    NPAD = NT * P
    LAST = NTOK - (NT - 1) * P
    KD = D // P
    NE = gate_w.shape[1]
    NEXP = NE + 1
    HC = w_ffn.shape[1]
    WROW = w_ffn.shape[3]
    UP = KD * P
    T = 256
    TB = T // P
    SH_TILES = cdiv(NTOK, T)
    MAX_TILES = SH_TILES + (TOPK * NTOK - NE) // T + NE
    MIN_TILES = SH_TILES + max(cdiv(TOPK * NTOK, T), NE)
    XS_TILES = MAX_TILES + 2
    MAXB = cdiv(NTOK, T)
    STAGE = 4
    NAB = 4
    NTB = 3
    LAG = 3
    GCOLS = [(c, min(512, NPAD - c)) for c in range(0, NPAD, 512)]
    NG = D + 1 + D + 2

    HALF = 6
    ROUTE = {HALF + 1 + s: (2 * s, 2 * s + 1) for s in range(HALF // 2)}
    ROUTE.update({NT + s: tuple(range(HALF + 2 * s, min(HALF + 2 * s + 2, NT))) for s in range(cdiv(NT - HALF, 2))})

    def before(j, ring):
        return max(c for c in range(HC) if c % ring == j % ring)

    xs = nc.dram_tensor("expert_inputs", [XS_TILES * T, D], F32, kind="Internal").ap()
    ys = nc.dram_tensor("expert_outputs", [MAX_TILES * T, D], F32, kind="Internal").ap()

    with ExitStack() as ctx:
        def sem(name):
            return ctx.enter_context(nc.semaphore(name))

        def sb(name, shape, dt=F32):
            return ctx.enter_context(nc.sbuf_tensor(name, shape, dt))

        xres = sb("xres", [P, NT, D])
        xn = sb("xn", [P, NT, D])
        ident = sb("ident", [P, P])
        tri = sb("tri", [P, P])
        ones = sb("ones", [P, P])
        tri_e = sb("tri_e", [P, NE, NE])
        valid = sb("valid", [P, 1])
        gatew = sb("gatew", [P, KD, NE])
        rbias = sb("rbias", [P, NE])
        gates = sb("gates", [P, NT, NE])
        rank = sb("rank", [P, NT, NE])
        chosen = sb("chosen", [P, NT, NE])
        seen = sb("seen", [P, NT + 1, NE])
        ntile = sb("ntile", [P, NE])
        tiles_to = sb("tiles_to", [P, NE])
        slot0 = sb("slot0", [P, NE])
        ones_e = sb("ones_e", [P, NE])
        slot = sb("slot", [P, NT, NE])
        pick = sb("pick", [P, NT, NE])
        slot_k = sb("slot_k", [P, TOPK, NT])
        slot_i = sb("slot_i", [P, TOPK, NT], U32)
        ntile_i = sb("ntile_i", [1, NE], I32)
        total_i = sb("total_i", [1, 1], I32)
        total_f = sb("total_f", [P, 1])
        gmax = sb("gmax", [P, NT])
        gexp = sb("gexp", [P, NT, NE])
        gsum = sb("gsum", [P, NT])
        weight_k = sb("weight_k", [P, TOPK, NT])
        stats = sb("stats", [P, NT, 6])
        mv = sb("mv", [P, NT, 2])
        rstd = sb("rstd", [P, NT])
        z = sb("z", [P, 2, D])
        small = sb("small", [P, NT, 4])
        xT2 = sb("xT2", [P, 2, KD, P])
        rk = sb("rk", [P, 2, NE, NE])
        zeros = sb("zeros", [P, D])

        graph = ExitStack()

        def gsb(name, shape, dt=F32):
            return graph.enter_context(nc.sbuf_tensor(name, shape, dt))

        adj_sb = gsb("adj_sb", [P, NT, NPAD])
        e_sb = gsb("e_sb", [P, NT, NPAD])
        XW = max(KD * NPAD, NT * (D + 2))
        xnT_xb = gsb("xnT_xb", [P, XW])
        xnT = xnT_xb[:, 0:KD * NPAD].rearrange("p (k t) -> p k t", k=KD)
        xb = xnT_xb[:, 0:NT * (D + 2)].rearrange("p (n c) -> p n c", n=NT)
        node = gsb("node", [P, NT, NG])
        srow = gsb("srow", [P, NPAD])
        cw = e_sb[:, 0, 0:KD * 2 * D].rearrange("p (k c) -> p k c", k=KD)
        wsT = e_sb[:, 1, 0:KD * D].rearrange("p (k c) -> p k c", k=KD)
        ub = e_sb[:, 2, 0:KD * P].rearrange("p (k c) -> p k c", k=KD)
        cv = e_sb[:, 3, 0:KD * 6].rearrange("p (k c) -> p k c", k=KD)
        ac = e_sb[:, 4, 0:KD * 2].rearrange("p (k c) -> p k c", k=KD)
        scol = gsb("scol", [P, NT, 4])
        abias = gsb("abias", [P, 2])
        gbias = gsb("gbias", [P, D])
        att = gsb("att", [P, NT, 2])
        graph.close()

        experts = ExitStack()

        def esb(name, shape, dt=F32):
            return experts.enter_context(nc.sbuf_tensor(name, shape, dt))

        WH = [esb(f"w_high{i}", [P, HC, WROW], F32R) for i in range(2)]
        WL = [esb(f"w_low{i}", [P, HC, WROW], F32R) for i in range(2)]
        stage = [esb(f"stage{i}", [P, WROW]) for i in range(STAGE)]
        xg = esb("xg", [P, TB, D])
        xTh = esb("xTh", [P, KD, T], F32R)
        xTl = esb("xTl", [P, KD, T], F32R)
        act_t = esb("act_t", [P, NTB, T])
        hid = esb("hid", [P, 2, T])
        hh = esb("hh", [P, NAB, T], F32R)
        hl = esb("hl", [P, NAB, T], F32R)
        ysb = esb("ysb", [P, TB, D])
        experts.close()

        final = ExitStack()
        FR = 4
        got = final.enter_context(nc.sbuf_tensor("got", [P, FR, TOPK, D], F32))
        ysh = final.enter_context(nc.sbuf_tensor("ysh", [P, FR, D], F32))
        outb = final.enter_context(nc.sbuf_tensor("outb", [P, FR, D], F32))
        final.close()

        ps = [ctx.enter_context(nc.psum_tensor(f"bank{i}", [P, 512], F32)) for i in range(8)]

        def whi(p, j, m, k):
            o = m * UP + k * P
            return WH[p][:, j, o:o + P]

        def wlo(p, j, m, k):
            o = m * UP + k * P
            return WL[p][:, j, o:o + P]

        x_in, par_in, adj_in, late_in = sem("x_in"), sem("par_in"), sem("adj_in"), sem("late_in")
        const_set = sem("const_set")
        masks = sem("masks")
        zeros_set = sem("zeros_set")
        dve_step = sem("dve_step")
        var_ready, std_ready = sem("var_ready"), sem("std_ready")
        xn1_ready = sem("xn1_ready")
        xnT_psum = sem("xnT_psum")
        xnT_ready = sem("xnT_ready")
        u_psum, u_ready = sem("u_psum"), sem("u_ready")
        node_psum = sem("node_psum")
        node_act, node_dve = sem("node_act"), sem("node_dve")
        srow_psum, srow_ready = sem("srow_psum"), sem("srow_ready")
        score_v, score_w, score_e, e_ready = sem("score_v"), sem("score_w"), sem("score_e"), sem("e_ready")
        xb_psum, xb_ready = sem("xb_psum"), sem("xb_ready")
        att_sum, att_ready = sem("att_sum"), sem("att_ready")
        xa_psum, z_ready, gn_ready = sem("xa_psum"), sem("z_ready"), sem("gn_ready")
        xn2_ready, xT2_psum, xT2_ready = sem("xn2_ready"), sem("xT2_psum"), sem("xT2_ready")
        gate_psum, chosen_ready, pos_psum = sem("gate_psum"), sem("chosen_ready"), sem("pos_psum")
        counts_ready, slots_ready = sem("counts_ready"), sem("slots_ready")
        gshift, gexp_ready = sem("gshift"), sem("gexp_ready")
        graph_free = sem("graph_free")
        rows_filled, rows_stored, scattered = sem("rows_filled"), sem("rows_stored"), sem("scattered")
        stage_in = [sem(f"stage_in{i}") for i in range(STAGE)]
        high_split, low_split = sem("high_split"), sem("low_split")
        x_loaded, xT_psum, xTh_ready, xT_ready = sem("x_loaded"), sem("xT_psum"), sem("xTh_ready"), sem("xT_ready")
        up_done, silu_done, h_done = sem("up_done"), sem("silu_done"), sem("h_done")
        hh_done, hl_ready, down_done = sem("hh_done"), sem("hl_ready"), sem("down_done")
        y_copied, y_stored = sem("y_copied"), sem("y_stored")
        all_stored = sem("all_stored")
        gathered = [sem(f"gathered{i}") for i in range(FR)]
        shared_in = [sem(f"shared_in{i}") for i in range(FR)]
        out_ready = sem("out_ready")
        out_stored = [sem(f"out_stored{i}") for i in range(FR)]

        N_PAR = 7
        FILLS = [(xs, r, min(4 * P, XS_TILES * T - r)) for r in range(NPAD, XS_TILES * T, 4 * P)]
        FILLS += [(ys, r, min(4 * P, MAX_TILES * T - r)) for r in range(MIN_TILES * T, MAX_TILES * T, 4 * P)]

        block = ctx.enter_context(nc.Block())

        @block.sync
        def _(sp):
            sp.dma_start(xres[:, :, :], x.rearrange("(n p) d -> p n d", p=P)).then_inc(x_in, 16)
            sp.dma_start(cw[:, :, 0:D], w_sa.rearrange("(k p) n -> p k n", p=P)).then_inc(par_in, 16)
            sp.dma_start(cw[:, :, D:2 * D], w_gcn.rearrange("(k p) n -> p k n", p=P)).then_inc(par_in, 16)
            sp.dma_start(wsT[:, :, :], w_saT.rearrange("(k p) n -> p k n", p=P)).then_inc(par_in, 16)
            sp.dma_start(ac[:, :, :], a_cols.rearrange("(k p) n -> p k n", p=P)).then_inc(par_in, 16)
            sp.dma_start(cv[:, :, 0:4], attn_cols.rearrange("(k p) n -> p k n", p=P)).then_inc(par_in, 16)
            sp.dma_start(gatew[:, :, :], gate_w.rearrange("(k p) n -> p k n", p=P)).then_inc(par_in, 16)
            sp.dma_start(gbias[:, :], gcn_bias.partition_broadcast(P)).then_inc(late_in, 16)
            sp.dma_start(abias[:, :], attn_bias.partition_broadcast(P)).then_inc(late_in, 16)
            sp.dma_start(rbias[:, :], routing_bias.partition_broadcast(P)).then_inc(late_in, 16)
            sp.dma_start(adj_sb[:, :, :], adjT.rearrange("(n p) i -> p n i", p=P)).then_inc(adj_in, 16)
            sp.wait_ge(zeros_set, 1)
            for rows, r, n in FILLS:
                sp.dma_start(rows[r:r + n, :].rearrange("(p q) d -> p q d", p=P),
                             zeros[:, :].unsqueeze(1).to_broadcast([P, n // P, D])).then_inc(rows_filled, 16)
            for n in range(NT):
                sp.wait_ge(xn2_ready, n + 1)
                sp.dma_start(xs[n * P:(n + 1) * P, :], xn[:, n, :]).then_inc(rows_stored, 16)
            sp.wait_ge(graph_free, 1)

            def load_expert(e, first):
                for j in range(HC):
                    if j >= STAGE:
                        sp.wait_ge(low_split, e * HC + (j - STAGE + 1))
                    elif not first:
                        sp.wait_ge(low_split, e * HC + (before(j, STAGE) + 1 - HC))
                    sp.dma_start(stage[j % STAGE][:, :], w_ffn[e, j, :, :] if first else
                                 w_ffn[bass.ds(e, 1), j, :, :].rearrange("e p n -> (e p) n"))\
                        .then_inc(stage_in[j % STAGE], 16)

            load_expert(0, True)
            with sp.Fori(1, NEXP) as e:
                load_expert(e, False)

            def store_out(n):
                rows = LAST if n == NT - 1 else P
                sp.wait_ge(out_ready, n + 1)
                sp.dma_start(out[n * P:n * P + rows, :], outb[0:rows, n % FR, :])\
                    .then_inc(out_stored[n % FR], 16)

            sp.wait_ge(counts_ready, 1)
            total = sp.value_load(total_i[0:1, 0:1], min_val=SH_TILES + NE, max_val=MAX_TILES)
            sp.wait_ge(x_loaded, total * 16 + 32)
            sp.wait_ge(y_stored, total * 16)
            sp.sem_inc(all_stored, 1)
            for n in range(NT):
                if n >= FR:
                    sp.wait_ge(out_ready, n - FR + 1)
                sp.dma_start(ysh[:, n % FR, :], ys[n * P:(n + 1) * P, :]).then_inc(shared_in[n % FR], 16)
                if n >= FR - 1:
                    store_out(n - FR + 1)
            for n in range(NT - FR + 1, NT):
                store_out(n)
            for r in range(FR):
                sp.wait_ge(out_stored[r], 16 * len(range(r, NT, FR)))

        @block.gpsimd
        def _(pool):
            pool.memset(zeros[:, :], 0.0).then_inc(zeros_set, 1)
            pool.memset(ident[:, :], 0.0).then_inc(const_set, 1)
            pool.memset(ones[:, :], 1.0).then_inc(const_set, 1)
            pool.memset(tri_e[:, :, :], 1.0).then_inc(const_set, 1)
            pool.memset(ones_e[:, :], 1.0).then_inc(const_set, 1)
            pool.wait_ge(const_set, 4)
            pool.affine_select(out=ident[:, :], in_=ident[:, :], compare_op=ALU.not_equal, fill=1.0,
                               base=0, pattern=[[-1, P]], channel_multiplier=1).then_inc(masks, 1)
            pool.affine_select(out=tri[:, :], in_=ones[:, :], compare_op=ALU.is_gt, fill=0.0,
                               base=0, pattern=[[1, P]], channel_multiplier=-1).then_inc(masks, 1)
            pool.affine_select(out=tri_e[:, :, :], in_=tri_e[:, :, :], compare_op=ALU.is_gt, fill=0.0,
                               base=0, pattern=[[1, NE], [-1, NE]], channel_multiplier=0)\
                .then_inc(masks, 1)
            pool.affine_select(out=valid[:, :], in_=ones[:, 0:1], compare_op=ALU.is_ge, fill=0.0,
                               base=LAST - 1, pattern=[[0, 1]], channel_multiplier=-1).then_inc(masks, 1)

            def split_low(e, p):
                for j in range(HC):
                    pool.wait_ge(high_split, e * HC + (j + 1))
                    pool.tensor_tensor(WL[p][:, j, :], stage[j % STAGE][:, :],
                                       WH[p][:, j, :].bitcast(F32), ALU.subtract).then_inc(low_split, 1)

            split_low(0, 0)
            split_low(1, 1)
            pool.wait_ge(slots_ready, 1)
            pool.wait_ge(rows_filled, 16 * len(FILLS))
            for n in range(NT):
                rows = LAST if n == NT - 1 else P
                for k in range(TOPK):
                    pool.indirect_dma_start(
                        out=xs[:, :], out_offset=bass.IndirectOffsetOnAxis(ap=slot_i[0:rows, k, n:n + 1], axis=0),
                        in_=xn[0:rows, n, :], in_offset=None).then_inc(scattered, 16)
            with pool.Fori(0, (NE - 2) // 2) as q:
                split_low(q * 2 + 2, 0)
                split_low(q * 2 + 3, 1)
            split_low(NEXP - 1, 0)

            pool.wait_ge(all_stored, 1)
            for n in range(NT):
                rows = LAST if n == NT - 1 else P
                if n >= FR:
                    pool.wait_ge(out_ready, n - FR + 1)
                for k in range(TOPK):
                    pool.indirect_dma_start(
                        out=got[0:rows, n % FR, k, :], out_offset=None, in_=ys[:, :],
                        in_offset=bass.IndirectOffsetOnAxis(ap=slot_i[0:rows, k, n:n + 1], axis=0))\
                        .then_inc(gathered[n % FR], 16)

        @block.scalar
        def _(act):
            act.wait_ge(var_ready, 1)
            act.activation(rstd[:, :], rstd[:, :], ACT.Sqrt).then_inc(std_ready, 1)
            for n in range(NT):
                act.wait_ge(xnT_psum, n + 1)
                act.activation(xnT[:, :, n * P:(n + 1) * P],
                               ps[n % 2][:, 0:KD * P].rearrange("p (k t) -> p k t", k=KD),
                               ACT.Copy).then_inc(xnT_ready, 1)
            for n in range(NT):
                act.wait_ge(node_psum, n + 1)
                act.activation(node[:, n, 0:D], ps[3 + n % 2][:, 0:D], ACT.Copy)
                act.activation(node[:, n, D + 1:2 * D + 1], ps[3 + n % 2][:, D:2 * D], ACT.Copy).then_inc(node_act, 1)
            for b, (c, w) in enumerate(GCOLS):
                act.wait_ge(srow_psum, b + 1)
                act.activation(srow[:, c:c + w], ps[b][:, 0:w], ACT.Copy).then_inc(srow_ready, 1)
            act.wait_ge(srow_ready, len(GCOLS))
            act.wait_ge(node_dve, NT)

            def score(n):
                act.activation(e_sb[:, n, :], srow[:, :], ACT.Identity, bias=scol[:, n, 3:4]).then_inc(score_v, 1)

            score(0)
            for n in range(NT):
                if n + 1 < NT:
                    score(n + 1)
                act.wait_ge(score_w, n + 1)
                act.activation(e_sb[:, n, :], e_sb[:, n, :], ACT.Exp, scale=-1.0).then_inc(score_e, 1)
                act.wait_ge(xb_psum, n + 1)
                act.activation(xb[:, n, :], ps[3 + n % 2][:, 0:D + 2], ACT.Copy).then_inc(xb_ready, 1)
            act.wait_ge(att_sum, 1)
            act.activation(att[:, :, :], att[:, :, :], ACT.Sigmoid).then_inc(att_ready, 1)
            for n in range(NT):
                act.wait_ge(z_ready, n + 1)
                act.activation(z[:, n % 2, :], z[:, n % 2, :], ACT.Sigmoid).then_inc(gn_ready, 1)
                if n in (HALF - 1, NT - 1):
                    part = slice(0, HALF) if n < HALF else slice(HALF, NT)
                    act.wait_ge(var_ready, 2 if n < HALF else 3)
                    act.activation(rstd[:, part], rstd[:, part], ACT.Sqrt).then_inc(std_ready, 1)
            act.wait_ge(gshift, 1)
            act.activation(gexp[:, :, :], gexp[:, :, :], ACT.Exp).then_inc(gexp_ready, 1)

            def split_high(e, p, j):
                uses = len(range(j % STAGE, HC, STAGE))
                act.wait_ge(stage_in[j % STAGE], e * (16 * uses) + 16 * (j // STAGE + 1))
                act.activation(WH[p][:, j, :], stage[j % STAGE][:, :], ACT.Copy).then_inc(high_split, 1)

            def load_x(g):
                act.dma_start(xg[:, :, :], xs[bass.ds(g * T, T), :].rearrange("(b p) d -> p b d", p=P))\
                    .then_inc(x_loaded, 16)

            def take_xT(g):
                act.wait_ge(xT_psum, g + 1)
                act.activation(xTh[:, :, :], ps[6][:, :].rearrange("p (k t) -> p k t", k=KD),
                               ACT.Copy).then_inc(xTh_ready, 1)

            def tile(g, first, prep):
                for j in range(HC):
                    act.wait_ge(up_done, g * HC + (j + 1))
                    if j >= NTB:
                        act.wait_ge(h_done, g * HC + (j - NTB + 1))
                    elif not first:
                        act.wait_ge(h_done, g * HC + (before(j, NTB) + 1 - HC))
                    act.activation(act_t[:, j % NTB, :], ps[j % NAB][:, 0:T], ACT.Silu).then_inc(silu_done, 1)
                    if prep is not None:
                        split_high(prep[0], prep[1], j)
                take_xT(g + 1)
                load_x(g + 2)
                act.wait_ge(down_done, g * HC + HC)
                if not first:
                    act.wait_ge(y_stored, g * 16)
                for b in range(TB):
                    act.activation(ysb[:, b, :], ps[4 + b][:, 0:D], ACT.Copy).then_inc(y_copied, 1)
                act.wait_ge(y_copied, g * TB + TB)
                act.dma_start(ys[bass.ds(g * T, T), :].rearrange("(b p) d -> p b d", p=P), ysb[:, :, :])\
                    .then_inc(y_stored, 16)

            act.wait_ge(graph_free, 1)
            for j in range(HC):
                split_high(0, 0, j)
                if j == 0:
                    act.wait_ge(rows_stored, 16 * NT)
                    act.wait_ge(rows_filled, 16 * len(FILLS))
                    load_x(0)
                if j == 2:
                    take_xT(0)
                    load_x(1)
            tile(0, True, (1, 1))
            with act.Fori(1, SH_TILES - 2) as g:
                tile(g, False, None)
            act.wait_ge(scattered, 16 * NT * TOPK)
            with act.Fori(SH_TILES - 2, SH_TILES) as g:
                tile(g, False, None)
            act.wait_ge(counts_ready, 1)
            gr = act.alloc_register("act_tile")
            act.reg_mov(gr, SH_TILES)

            def routed_tile(prep):
                tile(act.snap(gr, min_val=SH_TILES, max_val=MAX_TILES - 1), False, prep)
                act.reg_add(gr, gr, 1)

            def expert(e, nxt):
                n = act.value_load(ntile_i[0:1, bass.ds(e - 1, 1)], min_val=1, max_val=MAXB)
                routed_tile(nxt)
                with act.If(n > 1):
                    with act.Fori(1, n):
                        routed_tile(None)
                with act.Else():
                    pass

            with act.Fori(0, (NE - 2) // 2) as q:
                expert(q * 2 + 1, (q * 2 + 2, 0))
                expert(q * 2 + 2, (q * 2 + 3, 1))
            expert(NEXP - 2, (NEXP - 1, 0))
            expert(NEXP - 1, None)

        @block.vector
        def _(dve):
            steps = [0]

            def link(ins):
                steps[0] += 1
                ins.then_inc(dve_step, 1)
                dve.wait_ge(dve_step, steps[0])

            dve.wait_ge(x_in, 16)
            for n in range(NT):
                last = dve.bn_stats(stats[:, n, :], xres[:, n, :])
            link(last)
            for n in range(NT):
                last = dve.bn_aggr(mv[:, n, :], stats[:, n, :])
            link(last)
            dve.tensor_scalar(rstd[:, :], mv[:, :, 1], EPS, None, ALU.add).then_inc(var_ready, 1)
            dve.wait_ge(std_ready, 1)
            link(dve.reciprocal(rstd[:, :], rstd[:, :]))
            for n in range(NT):
                dve.tensor_scalar(xn[:, n, :], xres[:, n, :], mv[:, n, 0:1], rstd[:, n:n + 1],
                                  ALU.subtract, ALU.mult).then_inc(xn1_ready, 1)
            dve.memset(node[:, :, D:D + 1], 1.0)
            dve.wait_ge(u_psum, 1)
            uv = ps[2][:, 0:2 * KD].rearrange("p (k c) -> p k c", k=KD)
            link(dve.tensor_copy(cv[:, :, 4:6], uv))
            dve.tensor_copy(ub[:, :, :], cv[:, :, 4:5].to_broadcast([P, KD, P])).then_inc(u_ready, 1)
            for n in range(NT):
                dve.wait_ge(node_psum, n + 1)
                dve.tensor_copy(node[:, n, 2 * D + 1:NG], ps[5 + n % 2][:, 0:2])
                dve.tensor_copy(scol[:, n, :], ps[5 + n % 2][:, 2:6]).then_inc(node_dve, 1)
            dve.wait_ge(adj_in, 16)

            def mask(n):
                dve.wait_ge(score_e, n + 1)
                dve.scalar_tensor_tensor(out=e_sb[:, n, :], in0=adj_sb[:, n, :], scalar=0.0, in1=e_sb[:, n, :],
                                         op0=ALU.not_equal, op1=ALU.mult).then_inc(e_ready, 1)

            for n in range(NT):
                dve.wait_ge(score_v, n + 1)
                dve.scalar_tensor_tensor(out=e_sb[:, n, :], in0=e_sb[:, n, :], scalar=0.01, in1=e_sb[:, n, :],
                                         op0=ALU.mult, op1=ALU.max).then_inc(score_w, 1)
                if n:
                    mask(n - 1)
            mask(NT - 1)
            dve.wait_ge(xb_ready, NT)
            dve.wait_ge(late_in, 48)
            link(dve.tensor_tensor(att[:, :, :], xb[:, :, D:D + 2], scol[:, :, 0:2], ALU.add))
            dve.tensor_tensor(att[:, :, :], att[:, :, :], abias[:, :].unsqueeze(1).to_broadcast([P, NT, 2]),
                              ALU.add).then_inc(att_sum, 1)
            link(dve.tensor_tensor(xb[:, :, 0:D], xb[:, :, 0:D], gbias[:, :].unsqueeze(1).to_broadcast([P, NT, D]),
                                   ALU.add))
            dve.wait_ge(att_ready, 1)
            link(dve.tensor_tensor(xb[:, :, 0:D], xb[:, :, 0:D], att[:, :, 1:2].to_broadcast([P, NT, D]), ALU.mult))
            link(dve.memset(seen[:, 0, :], 0.0))

            def mix(n):
                pa = ps[n % 3]
                dve.wait_ge(xa_psum, n + 1)
                link(dve.tensor_scalar(small[:, n, 0:1], pa[:, D:D + 1], ATTN_EPS, None, ALU.add))
                link(dve.reciprocal(small[:, n, 1:2], small[:, n, 0:1]))
                link(dve.tensor_tensor(small[:, n, 2:3], small[:, n, 1:2], att[:, n, 0:1], ALU.mult))
                if n >= 2:
                    dve.wait_ge(gn_ready, n - 1)
                ins = dve.scalar_tensor_tensor(out=z[:, n % 2, :], in0=pa[:, 0:D], scalar=small[:, n, 2:3],
                                               in1=xb[:, n, 0:D], op0=ALU.mult, op1=ALU.add)
                ins.then_inc(z_ready, 1)

            def add_graph(n):
                dve.wait_ge(gn_ready, n + 1)
                link(dve.tensor_tensor(xres[:, n, :], xres[:, n, :], z[:, n % 2, :], ALU.add))
                link(dve.bn_stats(stats[:, n, :], xres[:, n, :]))
                link(dve.bn_aggr(mv[:, n, :], stats[:, n, :]))
                last = dve.tensor_scalar(rstd[:, n:n + 1], mv[:, n, 1:2], EPS, None, ALU.add)
                if n in (HALF - 1, NT - 1):
                    last.then_inc(var_ready, 1)

            def norm(n):
                if n in (0, HALF):
                    dve.wait_ge(std_ready, 2 if n == 0 else 3)
                    part = slice(0, HALF) if n == 0 else slice(HALF, NT)
                    link(dve.reciprocal(rstd[:, part], rstd[:, part]))
                dve.tensor_scalar(xn[:, n, :], xres[:, n, :], mv[:, n, 0:1], rstd[:, n:n + 1],
                                  ALU.subtract, ALU.mult).then_inc(xn2_ready, 1)

            def take_xT2(n):
                dve.wait_ge(xT2_psum, n + 1)
                dve.tensor_copy(xT2[:, n % 2, :, :], ps[3 + n % 2][:, 0:KD * P].rearrange("p (k t) -> p k t", k=KD))\
                    .then_inc(xT2_ready, 1)

            def route(n):
                dve.wait_ge(gate_psum, n + 1)
                link(dve.tensor_tensor(gates[:, n, :], ps[5 + n % 2][:, 0:NE], rbias[:, :], ALU.add))
                g = gates[:, n, :]
                other, own = g.unsqueeze(1).to_broadcast([P, NE, NE]), g.unsqueeze(2).to_broadcast([P, NE, NE])
                dve.tensor_tensor(rk[:, 0, :, :], other, own, ALU.is_gt)
                link(dve.tensor_tensor(rk[:, 1, :, :], other, own, ALU.is_equal))
                link(dve.tensor_tensor(rk[:, 1, :, :], rk[:, 1, :, :], tri_e[:, :, :], ALU.mult))
                link(dve.tensor_tensor(rk[:, 0, :, :], rk[:, 0, :, :], rk[:, 1, :, :], ALU.add))
                link(dve.tensor_reduce(rank[:, n, :], rk[:, 0, :, :], AX.X, ALU.add))
                if n < NT - 1:
                    link(dve.tensor_scalar(chosen[:, n, :], rank[:, n, :], float(TOPK), None, ALU.is_lt))
                else:
                    link(dve.tensor_scalar(chosen[:, n, :], rank[:, n, :], float(TOPK), valid[:, 0:1],
                                           ALU.is_lt, ALU.mult))
                dve.tensor_tensor(seen[:, n + 1, :], seen[:, n, :], chosen[:, n, :], ALU.add)\
                    .then_inc(chosen_ready, 1)
                dve.wait_ge(chosen_ready, n + 1)

            dve.wait_ge(masks, 4)
            for i in range(max(ROUTE) + 2):
                if i < NT:
                    mix(i)
                if i == NT - 1:
                    dve.wait_ge(z_ready, NT)
                    dve.sem_inc(graph_free, 1)
                if 1 <= i <= NT:
                    add_graph(i - 1)
                for t in ROUTE.get(i, ()):
                    norm(t)
                for t in ROUTE.get(i, ()):
                    take_xT2(t)
                for t in ROUTE.get(i - 1, ()):
                    route(t)
            dve.wait_ge(pos_psum, 1)
            count = ps[7][:, NT * NE:(NT + 1) * NE]
            link(dve.tensor_scalar(ntile[:, :], count, float(T), 1.0, ALU.is_gt, ALU.add))
            for b in range(2, MAXB):
                link(dve.scalar_tensor_tensor(out=ntile[:, :], in0=count, scalar=float(b * T), in1=ntile[:, :],
                                              op0=ALU.is_gt, op1=ALU.add))
            link(dve.tensor_tensor_scan(tiles_to[:, :], ones_e[:, :], ntile[:, :], 0.0, ALU.mult, ALU.add))
            link(dve.tensor_scalar(total_f[:, :], tiles_to[:, NE - 1:NE], float(SH_TILES), None, ALU.add))
            dve.tensor_copy(ntile_i[:, :], ntile[0:1, :])
            dve.tensor_copy(total_i[:, :], total_f[0:1, :]).then_inc(counts_ready, 1)
            link(dve.tensor_tensor(slot0[:, :], tiles_to[:, :], ntile[:, :], ALU.subtract))
            link(dve.tensor_scalar(slot0[:, :], slot0[:, :], float(SH_TILES), float(T), ALU.add, ALU.mult))
            link(dve.tensor_tensor(slot[:, :, :], ps[7][:, 0:NT * NE].rearrange("p (n e) -> p n e", n=NT),
                                   slot0[:, :].unsqueeze(1).to_broadcast([P, NT, NE]), ALU.add))
            for k in range(TOPK):
                link(dve.scalar_tensor_tensor(out=pick[:, :, :], in0=rank[:, :, :], scalar=float(k), in1=slot[:, :, :],
                                              op0=ALU.is_equal, op1=ALU.mult))
                link(dve.tensor_reduce(slot_k[:, k, :], pick[:, :, :], AX.X, ALU.add))
            dve.tensor_copy(slot_i[:, :, :], slot_k[:, :, :]).then_inc(slots_ready, 1)
            link(dve.tensor_reduce(gmax[:, :], gates[:, :, :], AX.X, ALU.max))
            dve.tensor_tensor(gexp[:, :, :], gates[:, :, :], gmax[:, :].unsqueeze(2).to_broadcast([P, NT, NE]),
                              ALU.subtract).then_inc(gshift, 1)

            def softmax():
                dve.wait_ge(gexp_ready, 1)
                for k in range(TOPK):
                    link(dve.scalar_tensor_tensor(out=pick[:, :, :], in0=rank[:, :, :], scalar=float(k),
                                                  in1=gexp[:, :, :], op0=ALU.is_equal, op1=ALU.mult))
                    link(dve.tensor_reduce(weight_k[:, k, :], pick[:, :, :], AX.X, ALU.add))
                link(dve.tensor_tensor(gsum[:, :], weight_k[:, 0, :], weight_k[:, 1, :], ALU.add))
                link(dve.tensor_tensor(gsum[:, :], gsum[:, :], weight_k[:, 2, :], ALU.add))
                link(dve.tensor_tensor(gsum[:, :], gsum[:, :], weight_k[:, 3, :], ALU.add))
                link(dve.reciprocal(gsum[:, :], gsum[:, :]))
                link(dve.tensor_tensor(weight_k[:, :, :], weight_k[:, :, :],
                                       gsum[:, :].unsqueeze(1).to_broadcast([P, TOPK, NT]), ALU.mult))

            def take_xT(g):
                dve.wait_ge(xTh_ready, g + 1)
                dve.tensor_tensor(xTl[:, :, :], ps[6][:, :].rearrange("p (k t) -> p k t", k=KD),
                                  xTh[:, :, :].bitcast(F32), ALU.subtract).then_inc(xT_ready, 1)

            def tile(g, first):
                for j in range(HC):
                    dve.wait_ge(silu_done, g * HC + (j + 1))
                    dve.tensor_tensor(hid[:, j % 2, :], act_t[:, j % NTB, :], ps[j % NAB][:, T:2 * T], ALU.mult)\
                        .then_inc(h_done, 1)
                    dve.wait_ge(h_done, g * HC + (j + 1))
                    if j >= NAB:
                        dve.wait_ge(down_done, g * HC + (j - NAB + 1))
                    elif not first:
                        dve.wait_ge(down_done, g * HC + (before(j, NAB) + 1 - HC))
                    dve.tensor_copy(hh[:, j % NAB, :], hid[:, j % 2, :]).then_inc(hh_done, 1)
                    dve.wait_ge(hh_done, g * HC + (j + 1))
                    dve.tensor_tensor(hl[:, j % NAB, :], hid[:, j % 2, :], hh[:, j % NAB, :].bitcast(F32),
                                      ALU.subtract).then_inc(hl_ready, 1)
                take_xT(g + 1)

            take_xT(0)
            tile(0, True)
            softmax()
            with dve.Fori(1, SH_TILES) as g:
                tile(g, False)
            gr = dve.alloc_register("dve_tile")
            dve.reg_mov(gr, SH_TILES)

            def routed_tile():
                tile(dve.snap(gr, min_val=SH_TILES, max_val=MAX_TILES - 1), False)
                dve.reg_add(gr, gr, 1)

            dve.wait_ge(counts_ready, 1)
            with dve.Fori(0, NE) as e:
                n = dve.value_load(ntile_i[0:1, bass.ds(e, 1)], min_val=1, max_val=MAXB)
                with dve.Fori(0, n):
                    routed_tile()

            for n in range(NT):
                dve.wait_ge(shared_in[n % FR], 16 * (n // FR + 1))
                dve.wait_ge(gathered[n % FR], 16 * TOPK * (n // FR + 1))
                if n >= FR:
                    dve.wait_ge(out_stored[n % FR], 16 * (n // FR))
                rows = LAST if n == NT - 1 else P
                link(dve.tensor_tensor(outb[0:rows, n % FR, :], xres[0:rows, n, :], ysh[0:rows, n % FR, :], ALU.add))
                for k in range(TOPK):
                    last = dve.scalar_tensor_tensor(out=outb[0:rows, n % FR, :], in0=got[0:rows, n % FR, k, :],
                                                    scalar=weight_k[0:rows, k, n:n + 1], in1=outb[0:rows, n % FR, :],
                                                    op0=ALU.mult, op1=ALU.add)
                    if k < TOPK - 1:
                        link(last)
                last.then_inc(out_ready, 1)

        @block.tensor
        def _(pe):
            pe.wait_ge(masks, 1)
            pe.wait_ge(par_in, 16 * 6)
            for c in range(KD):
                for k in range(KD):
                    last = pe.matmul(ps[2][:, 2 * c:2 * c + 2], wsT[:, k, c * P:(c + 1) * P], ac[:, k, :],
                                     start=(k == 0), stop=(k == KD - 1))
            last.then_inc(u_psum, 1)
            for n in range(NT):
                pe.wait_ge(xn1_ready, n + 1)
                if n >= 2:
                    pe.wait_ge(xnT_ready, n - 1)
                for k in range(KD):
                    last = pe.transpose(ps[n % 2][:, k * P:(k + 1) * P], xn[:, n, k * P:(k + 1) * P], ident[:, :])
                last.then_inc(xnT_psum, 1)
            pe.wait_ge(u_ready, 1)
            for n in range(NT):
                pe.wait_ge(xnT_ready, n + 1)
                if n >= 2:
                    pe.wait_ge(node_act, n - 1)
                    pe.wait_ge(node_dve, n - 1)
                for k in range(KD):
                    pe.matmul(ps[3 + n % 2][:, :], xnT[:, k, n * P:(n + 1) * P], cw[:, k, :],
                              start=(k == 0), stop=(k == KD - 1))
                for k in range(KD):
                    last = pe.matmul(ps[5 + n % 2][:, 0:6], xnT[:, k, n * P:(n + 1) * P], cv[:, k, :],
                                     start=(k == 0), stop=(k == KD - 1))
                last.then_inc(node_psum, 1)
            for b, (c, w) in enumerate(GCOLS):
                for k in range(KD):
                    last = pe.matmul(ps[b][:, 0:w], ub[:, k, :], xnT[:, k, c:c + w],
                                     start=(k == 0), stop=(k == KD - 1))
                last.then_inc(srow_psum, 1)
            pe.wait_ge(adj_in, 16)
            pe.wait_ge(node_act, NT)
            pe.wait_ge(node_dve, NT)
            for i in range(NT):
                if i >= 2:
                    pe.wait_ge(xb_ready, i - 1)
                for n in range(NT):
                    last = pe.matmul(ps[3 + i % 2][:, 0:D + 2], adj_sb[:, n, i * P:(i + 1) * P], node[:, n, D + 1:NG],
                                     start=(n == 0), stop=(n == NT - 1))
                last.then_inc(xb_psum, 1)
            for i in range(max(ROUTE) + 3):
                if i < NT:
                    if i == 0:
                        pe.wait_ge(srow_ready, len(GCOLS))
                        pe.wait_ge(xb_ready, NT)
                    if i >= 3:
                        pe.wait_ge(z_ready, i - 2)
                    for n in range(NT):
                        if i == 0:
                            pe.wait_ge(e_ready, n + 1)
                        last = pe.matmul(ps[i % 3][:, 0:D + 1], e_sb[:, n, i * P:(i + 1) * P], node[:, n, 0:D + 1],
                                         start=(n == 0), stop=(n == NT - 1))
                    last.then_inc(xa_psum, 1)
                for t in ROUTE.get(i - 1, ()):
                    pe.wait_ge(xT2_ready, t + 1)
                    if t >= 2:
                        pe.wait_ge(chosen_ready, t - 1)
                    for k in range(KD):
                        last = pe.matmul(ps[5 + t % 2][:, 0:NE], xT2[:, t % 2, k, :], gatew[:, k, :],
                                         start=(k == 0), stop=(k == KD - 1))
                    last.then_inc(gate_psum, 1)
                for t in ROUTE.get(i, ()):
                    pe.wait_ge(xn2_ready, t + 1)
                    if t >= 2:
                        pe.wait_ge(xT2_ready, t - 1)
                    for k in range(KD):
                        last = pe.transpose(ps[3 + t % 2][:, k * P:(k + 1) * P], xn[:, t, k * P:(k + 1) * P], ident[:, :])
                    last.then_inc(xT2_psum, 1)
                for t in ROUTE.get(i - 2, ()):
                    if t == 0:
                        pe.wait_ge(masks, 4)
                    pe.wait_ge(chosen_ready, t + 1)
                    pe.matmul(ps[7][:, t * NE:(t + 1) * NE], tri[:, :], chosen[:, t, :], start=True, stop=False)
                    pe.matmul(ps[7][:, t * NE:(t + 1) * NE], ones[:, :], seen[:, t, :], start=False, stop=True)
            pe.matmul(ps[7][:, NT * NE:(NT + 1) * NE], ones[:, :], seen[:, NT, :], start=True, stop=True)\
                .then_inc(pos_psum, 1)

            def transpose_x(g):
                pe.wait_ge(x_loaded, g * 16 + 16)
                for k in range(KD):
                    for b in range(TB):
                        last = pe.transpose(ps[6][:, k * T + b * P:k * T + (b + 1) * P],
                                            xg[:, b, k * P:(k + 1) * P], ident[:, :])
                last.then_inc(xT_psum, 1)

            def up(p, j):
                for m in range(2):
                    o = ps[j % NAB][:, m * T:(m + 1) * T]
                    for k in range(KD):
                        pe.matmul(o, whi(p, j, m, k), xTh[:, k, :], start=(k == 0), stop=False)
                        pe.matmul(o, whi(p, j, m, k), xTl[:, k, :], start=False, stop=False)
                        last = pe.matmul(o, wlo(p, j, m, k), xTh[:, k, :], start=False, stop=(k == KD - 1))
                last.then_inc(up_done, 1)

            def down(g, p, j, first):
                pe.wait_ge(hl_ready, g * HC + (j + 1))
                if j == 0 and not first:
                    pe.wait_ge(y_copied, g * TB)
                hi, lo = WH[p][:, j, 2 * UP:2 * UP + D], WL[p][:, j, 2 * UP:2 * UP + D]
                for n, (h, w) in enumerate(((hh, hi), (hh, lo), (hl, hi))):
                    for b in range(TB):
                        last = pe.matmul(ps[4 + b][:, 0:D], h[:, j % NAB, b * P:(b + 1) * P], w,
                                         start=(j == 0 and n == 0), stop=(j == HC - 1 and n == 2))
                last.then_inc(down_done, 1)

            def tile(g, p, first, e):
                pe.wait_ge(xT_ready, g + 1)
                for j in range(HC):
                    if e is not None:
                        pe.wait_ge(low_split, e * HC + (j + 1))
                    if j >= NAB:
                        pe.wait_ge(h_done, g * HC + (j - NAB + 1))
                    elif not first:
                        pe.wait_ge(h_done, g * HC + (before(j, NAB) + 1 - HC))
                    up(p, j)
                    if j >= LAG:
                        down(g, p, j - LAG, first)
                transpose_x(g + 1)
                for j in range(HC - LAG, HC):
                    down(g, p, j, first)

            transpose_x(0)
            tile(0, 0, True, 0)
            with pe.Fori(1, SH_TILES) as g:
                tile(g, 0, False, None)
            gr = pe.alloc_register("pe_tile")
            pe.reg_mov(gr, SH_TILES)

            def routed_tile(p, e):
                tile(pe.snap(gr, min_val=SH_TILES, max_val=MAX_TILES - 1), p, False, e)
                pe.reg_add(gr, gr, 1)

            def expert(e, p):
                n = pe.value_load(ntile_i[0:1, bass.ds(e - 1, 1)], min_val=1, max_val=MAXB)
                routed_tile(p, e)
                with pe.If(n > 1):
                    with pe.Fori(1, n):
                        routed_tile(p, None)
                with pe.Else():
                    pass

            pe.wait_ge(counts_ready, 1)
            with pe.Fori(0, (NE - 2) // 2) as q:
                expert(q * 2 + 1, 1)
                expert(q * 2 + 2, 0)
            expert(NEXP - 2, 1)
            expert(NEXP - 1, 0)


def _layout(inputs):
    import numpy as np

    a = {k: np.asarray(v) for k, v in inputs.items()}
    n, d = a["x"].shape
    pad = cdiv(n, P) * P
    x = np.zeros((pad, d), a["x"].dtype)
    x[:n] = a["x"]
    adj = np.zeros((pad, pad), a["adj"].dtype)
    adj[:n, :n] = a["adj"].T
    wa, wb, a_sa = a["L0_gnn_Wa"], a["L0_gnn_Wb"], a["L0_gnn_a_sa"]
    w1 = np.concatenate([a["L0_ffn_sw1"][None], a["L0_ffn_w1"]])
    w2 = np.concatenate([a["L0_ffn_sw2"][None], a["L0_ffn_w2"]])
    w3 = np.concatenate([a["L0_ffn_sw3"][None], a["L0_ffn_w3"]])
    ne, _, h = w1.shape
    hc = cdiv(h, P)

    def wide(w, axis):
        widths = [(0, 0)] * 3
        widths[axis] = (0, hc * P - h)
        return np.pad(w, widths)

    def up(w):
        return wide(w, 2).reshape(ne, d // P, P, hc, P).transpose(0, 3, 2, 1, 4).reshape(ne, hc, P, d)

    down = wide(w3, 1).reshape(ne, hc, P, d)
    return {
        "x": x,
        "adjT": adj,
        "w_sa": a["L0_gnn_W_sa"],
        "w_saT": a["L0_gnn_W_sa"].T,
        "w_gcn": a["L0_gnn_W_gcnb"],
        "a_cols": a_sa.reshape(2, d).T,
        "attn_cols": np.stack([wa[0, :d], wb[0, :d], wa[0, d:], wb[0, d:]], axis=1),
        "attn_bias": np.concatenate([a["L0_gnn_ba"], a["L0_gnn_bb"]]),
        "gcn_bias": a["L0_gnn_b_gcnb"],
        "gate_w": a["L0_ffn_gate_w"],
        "routing_bias": a["L0_ffn_routing_bias"],
        "w_ffn": np.concatenate([up(w1), up(w2), down], axis=3),
    }


def kernel(**inputs):
    import numpy as np
    import concourse.bacc as bacc
    from concourse.bass_utils import run_bass_kernel_spmd

    shape = np.asarray(inputs["x"]).shape
    nc = bacc.Bacc("TRN2", target_bir_lowering=False, num_devices=1)
    arrays, args = {}, []
    for name, a in _layout(inputs).items():
        arrays[f"in_{name}"] = np.ascontiguousarray(a)
        args.append(nc.dram_tensor(f"in_{name}", a.shape, mybir.dt.from_np(a.dtype), kind="ExternalInput").ap())
    out = nc.dram_tensor("out", shape, F32, kind="ExternalOutput").ap()
    graph_attention_and_routed_experts(nc, *args, out)
    r = run_bass_kernel_spmd(nc, [arrays], core_ids=[0])
    return r.results[0]["out"]
```

```python
from contextlib import ExitStack

import concourse.bass as bass
from concourse import mybir

F32 = mybir.dt.float32
F32R = mybir.dt.float32r
U32 = mybir.dt.uint32
I32 = mybir.dt.int32
ALU = mybir.AluOpType
ACT = mybir.ActivationFunctionType
AX = mybir.AxisListType

P = 128
EPS = 1e-5
ATTN_EPS = 1e-5
TOPK = 4


def cdiv(a, b):
    return -(-a // b)


def up_groups(hidden):
    whole = hidden // 512
    groups = [(512 * i, 512) for i in range(whole)]
    rest = cdiv(hidden - 512 * whole, 4) * 4
    return groups + [(512 * whole, max(rest, 256))]


def weight_pieces(hidden, d):
    groups = up_groups(hidden)
    return [2 * w for _, w in groups for _ in range(d // P)] + [cdiv(w, P) * d for _, w in groups]


def graph_attention_and_routed_experts(nc, x, adjT, w_sa, w_saT, w_gcn, a_cols, attn_cols,
                                       attn_bias, gcn_bias, gate_w, routing_bias, w_ffn, hidden, out):
    NTOK, D = out.shape
    NT = x.shape[0] // P
    NPAD = NT * P
    LAST = NTOK - (NT - 1) * P
    KD = D // P
    NE = gate_w.shape[1]
    NEXP = NE + 1
    UPS = up_groups(hidden)
    NG = len(UPS)
    GCH = 512 // P
    CHUNKS = [cdiv(w, P) for _, w in UPS]
    PIECES = weight_pieces(hidden, D)
    NPC = len(PIECES)
    WCOLS = sum(PIECES)
    AT = [sum(PIECES[:j]) for j in range(NPC)]
    EVEN, ODD = (NPC + 1) // 2, NPC // 2
    MAX_ROUTED = (TOPK * NTOK - NE) // P + NE
    MIN_ROUTED = max(cdiv(TOPK * NTOK, P), NE)
    XS_TILES = MAX_ROUTED + 2
    MAXB = NT
    PW = D + 1 + NE
    STAGE = 5
    CC = D + 1 + D + 2
    HALF = 6
    ROUTE = {HALF + 1 + s: (2 * s, 2 * s + 1) for s in range(HALF // 2)}
    ROUTE.update({NT + s: tuple(range(HALF + 2 * s, min(HALF + 2 * s + 2, NT))) for s in range(cdiv(NT - HALF, 2))})

    def before(j, ring):
        return max(c for c in range(NPC) if c % ring == j % ring)

    xs = nc.dram_tensor("expert_inputs", [XS_TILES * P, PW], F32, kind="Internal").ap()
    sums = nc.dram_tensor("token_sums", [NPAD + P, D], F32, kind="Internal").ap()

    with ExitStack() as ctx:
        def sem(name):
            return ctx.enter_context(nc.semaphore(name))

        def sb(name, shape, dt=F32):
            return ctx.enter_context(nc.sbuf_tensor(name, shape, dt))

        xres = sb("xres", [P, NT, D])
        xn = sb("xn", [P, NT, PW])
        ident = sb("ident", [P, P])
        tri = sb("tri", [P, P])
        ones = sb("ones", [P, P])
        valid = sb("valid", [P, 1])
        gatew = sb("gatew", [P, KD, NE])
        rbias = sb("rbias", [P, NE])
        iota_n = sb("iota_n", [P, NT], I32)
        iota_e = sb("iota_e", [P, NE], I32)
        iota_b = sb("iota_b", [P, MAXB - 1], I32)
        iota_p = sb("iota_p", [P, 1], I32)
        number_e = sb("number_e", [P, NE])
        number_b = sb("number_b", [P, MAXB - 1])
        gates = sb("gates", [P, NT, NE])
        top = sb("top", [P, NT, 8])
        top_i = sb("top_i", [P, NT, 8], U32)
        top_f = sb("top_f", [P, NT, TOPK])
        onehot = sb("onehot", [P, TOPK, NT, NE])
        pick = sb("pick", [P, TOPK, NT, NE])
        chosen = sb("chosen", [P, NT, NE])
        base = sb("base", [P, NT + 1, NE])
        above = sb("above", [P, NE, MAXB - 1])
        ntile = sb("ntile", [P, NE])
        tiles_to = sb("tiles_to", [P, NE])
        slot0 = sb("slot0", [P, NE])
        ones_e = sb("ones_e", [P, NE])
        slot = sb("slot", [P, NT, NE])
        slot_k = sb("slot_k", [P, TOPK, NT])
        slot_i = sb("slot_i", [P, TOPK, NT], U32)
        ntile_i = sb("ntile_i", [1, NE], I32)
        total_i = sb("total_i", [1, 1], I32)
        total_f = sb("total_f", [P, 1])
        gsum = sb("gsum", [P, NT])
        stats = sb("stats", [P, NT, 6])
        mv = sb("mv", [P, NT, 2])
        rstd = sb("rstd", [P, NT])
        small = sb("small", [P, NT, 4])

        graph = ExitStack()

        def gsb(name, shape, dt=F32):
            return graph.enter_context(nc.sbuf_tensor(name, shape, dt))

        adj_sb = gsb("adj_sb", [P, NT, NPAD])
        node = gsb("node", [P, NT, CC])
        xb = gsb("xb", [P, NT, D + 2])
        srow = gsb("srow", [P, NPAD])
        scol = gsb("scol", [P, NT, 4])
        z = gsb("z", [P, 2, D])
        xT2 = gsb("xT2", [P, 2, KD, P])
        fill = gsb("fill", [P, PW])
        abias = gsb("abias", [P, 2])
        gbias = gsb("gbias", [P, D])
        att = gsb("att", [P, NT, 2])
        rows = ExitStack()

        def rsb(name, shape, dt=F32):
            return rows.enter_context(nc.sbuf_tensor(name, shape, dt))

        xnTh = rsb("xnTh", [P, KD, NPAD], F32R)
        xnTl = rsb("xnTl", [P, KD, NPAD], F32R)
        cw = rsb("cw", [P, KD, 2 * D])
        cwh = rsb("cwh", [P, KD, 2 * D], F32R)
        cwl = rsb("cwl", [P, KD, 2 * D], F32R)
        cv = rsb("cv", [P, KD, 6])
        wsT = rsb("wsT", [P, KD, D])
        ac = rsb("ac", [P, KD, 2])
        srep = rsb("srep", [P, 2, P])
        rows.close()
        e_sb = gsb("e_sb", [P, NT, NPAD])
        graph.close()

        experts = ExitStack()

        def esb(name, shape, dt=F32):
            return experts.enter_context(nc.sbuf_tensor(name, shape, dt))

        WH = [esb(f"w_high{i}", [P, WCOLS], F32R) for i in range(2)]
        WL = [esb(f"w_low{i}", [P, WCOLS], F32R) for i in range(2)]
        stage = [esb(f"stage{i}", [P, max(PIECES)]) for i in range(STAGE)]
        xg = esb("xg", [P, PW])
        xTh = esb("xTh", [P, KD, P], F32R)
        xTl = esb("xTl", [P, KD, P], F32R)
        hid = esb("hid", [P, NG, 512])
        hh = esb("hh", [P, 2, 512], F32R)
        hl = esb("hl", [P, 2, 512], F32R)
        ysb = esb("ysb", [P, D])
        meta = esb("meta", [P, PW - D])
        dest = esb("dest", [P, 1], U32)
        wcol = esb("wcol", [P, 1])
        experts.close()

        ps = [ctx.enter_context(nc.psum_tensor(f"bank{i}", [P, 512], F32)) for i in range(8)]
        A_BANK, B_BANK, H_BANK, X_BANK, Y_BANK = (0, 2, 0), (1, 3, 1), (4, 5, 4), 6, 7

        x_in, par_in, adj_in, late_in = sem("x_in"), sem("par_in"), sem("adj_in"), sem("late_in")
        const_set, masks, numbers = sem("const_set"), sem("masks"), sem("numbers")
        dve_step = sem("dve_step")
        var_ready, std_ready = sem("var_ready"), sem("std_ready")
        xn1_ready, xnT_psum, xnTh_ready, xnT_ready = (
            sem("xn1_ready"), sem("xnT_psum"), sem("xnTh_ready"), sem("xnT_ready"))
        u_psum, u_ready, cwh_ready, cw_ready = sem("u_psum"), sem("u_ready"), sem("cwh_ready"), sem("cw_ready")
        node_psum, node_act, node_dve = sem("node_psum"), sem("node_act"), sem("node_dve")
        srep_ready, srow_psum, srow_ready = sem("srep_ready"), sem("srow_psum"), sem("srow_ready")
        score_v, score_w, score_e, e_ready = sem("score_v"), sem("score_w"), sem("score_e"), sem("e_ready")
        xb_psum, xb_ready = sem("xb_psum"), sem("xb_ready")
        att_sum, att_ready = sem("att_sum"), sem("att_ready")
        xa_psum, z_ready, gn_ready = sem("xa_psum"), sem("z_ready"), sem("gn_ready")
        xn2_ready, xT2_psum, xT2_ready = sem("xn2_ready"), sem("xT2_psum"), sem("xT2_ready")
        gate_psum, gate_read, chosen_ready, pos_psum = (
            sem("gate_psum"), sem("gate_read"), sem("chosen_ready"), sem("pos_psum"))
        counts_ready, slots_ready = sem("counts_ready"), sem("slots_ready")
        gshift, gexp_ready = sem("gshift"), sem("gexp_ready")
        graph_free = sem("graph_free")
        rows_filled = sem("rows_filled")
        stage_in = [sem(f"stage_in{i}") for i in range(STAGE)]
        high_dve, high_act, low_dve, low_pool = sem("high_dve"), sem("high_act"), sem("low_dve"), sem("low_pool")
        x_loaded, xT_psum, xTh_ready, xT_ready = sem("x_loaded"), sem("xT_psum"), sem("xTh_ready"), sem("xT_ready")
        up_done, silu_done, h_done, hT_psum = sem("up_done"), sem("silu_done"), sem("h_done"), sem("hT_psum")
        hh_ready, hl_ready, down_done = sem("hh_ready"), sem("hl_ready"), sem("down_done")
        meta_read, meta_ready = sem("meta_read"), sem("meta_ready")
        y_taken, y_stored, out_stored = sem("y_taken"), sem("y_stored"), sem("out_stored")
        rows_moved = sem("rows_moved")
        SCATTERS = NT * TOPK

        FILLS = [(r, min(4, XS_TILES - r)) for r in range(0, XS_TILES, 4)]

        def low_wait(eng, e, j):
            if isinstance(e, int) and e == 0:
                eng.wait_ge(low_dve if j % 2 == 0 else low_pool, j // 2 + 1)
            else:
                eng.wait_ge(low_pool, e * NPC + (j + 1 + ODD - NPC))

        def stage_wait(eng, e, j):
            uses = len(range(j % STAGE, NPC, STAGE))
            eng.wait_ge(stage_in[j % STAGE], e * (16 * uses) + 16 * (j // STAGE + 1))

        def piece(buf, j):
            return buf[:, AT[j]:AT[j] + PIECES[j]]

        def raw(j):
            return stage[j % STAGE][:, 0:PIECES[j]]

        block = ctx.enter_context(nc.Block())

        @block.sync
        def _(sp):
            sp.dma_start(xres[:, :, :], x.rearrange("(n p) d -> p n d", p=P)).then_inc(x_in, 16)
            sp.dma_start(cw[:, :, 0:D], w_sa.rearrange("(k p) n -> p k n", p=P)).then_inc(par_in, 16)
            sp.dma_start(cw[:, :, D:2 * D], w_gcn.rearrange("(k p) n -> p k n", p=P)).then_inc(par_in, 16)
            sp.dma_start(wsT[:, :, :], w_saT.rearrange("(k p) n -> p k n", p=P)).then_inc(par_in, 16)
            sp.dma_start(ac[:, :, :], a_cols.rearrange("(k p) n -> p k n", p=P)).then_inc(par_in, 16)
            sp.dma_start(cv[:, :, 0:4], attn_cols.rearrange("(k p) n -> p k n", p=P)).then_inc(par_in, 16)
            sp.dma_start(gatew[:, :, :], gate_w.rearrange("(k p) n -> p k n", p=P)).then_inc(par_in, 16)
            sp.dma_start(adj_sb[:, :, :], adjT.rearrange("(n p) i -> p n i", p=P)).then_inc(adj_in, 16)
            sp.dma_start(gbias[:, :], gcn_bias.partition_broadcast(P)).then_inc(late_in, 16)
            sp.dma_start(abias[:, :], attn_bias.partition_broadcast(P)).then_inc(late_in, 16)
            sp.dma_start(rbias[:, :], routing_bias.partition_broadcast(P)).then_inc(late_in, 16)
            sp.wait_ge(numbers, 6)
            for r, n in FILLS:
                sp.dma_start(xs[r * P:(r + n) * P, :].rearrange("(q p) d -> p q d", p=P),
                             fill[:, :].unsqueeze(1).to_broadcast([P, n, PW])).then_inc(rows_filled, 16)
            sp.dma_start(sums[NPAD:NPAD + P, :], fill[:, 0:D]).then_inc(y_stored, 16)
            sp.wait_ge(rows_filled, 16 * len(FILLS))
            sp.wait_ge(y_stored, 16)
            sp.wait_ge(graph_free, 1)

            def load_expert(e):
                for j in range(NPC):
                    if j >= STAGE:
                        low_wait(sp, e, j - STAGE)
                    elif not (isinstance(e, int) and e == 0):
                        low_wait(sp, e - 1, before(j, STAGE))
                    src = w_ffn[e, :, AT[j]:AT[j] + PIECES[j]] if isinstance(e, int) else \
                        w_ffn[bass.ds(e, 1), :, AT[j]:AT[j] + PIECES[j]].rearrange("e p n -> (e p) n")
                    sp.dma_start(raw(j), src).then_inc(stage_in[j % STAGE], 16)

            load_expert(0)
            load_expert(1)
            with sp.Fori(2, NEXP) as e:
                load_expert(e)
            sp.wait_ge(counts_ready, 1)
            total = sp.value_load(total_i[0:1, 0:1], min_val=NT + NE, max_val=NT + MAX_ROUTED)
            all_loaded, all_added = sp.alloc_register("all_loaded"), sp.alloc_register("all_added")
            sp.reg_mov(all_loaded, total * 16 + 16)
            sp.reg_mov(all_added, total * 16 + 16 * (SCATTERS - NT))
            sp.wait_ge(x_loaded, all_loaded)
            sp.wait_ge(rows_moved, all_added)
            flat = "t d -> (t d)"
            sp.dma_start(out.rearrange(flat).rearrange("(a b) -> a b", a=16),
                         sums[0:NTOK, :].rearrange(flat).rearrange("(a b) -> a b", a=16)).then_inc(out_stored, 16)
            sp.wait_ge(out_stored, 16)

        @block.gpsimd
        def _(pool):
            pool.memset(ident[:, :], 0.0).then_inc(const_set, 1)
            pool.memset(ones[:, :], 1.0).then_inc(const_set, 1)
            pool.memset(fill[:, :], 0.0).then_inc(const_set, 1)
            pool.memset(ones_e[:, :], 1.0).then_inc(const_set, 1)
            pool.iota(iota_n[:, :], pattern=[[P, NT]], base=0, channel_multiplier=1).then_inc(const_set, 1)
            pool.iota(iota_e[:, :], pattern=[[1, NE]], base=0, channel_multiplier=0).then_inc(const_set, 1)
            pool.iota(iota_b[:, :], pattern=[[P, MAXB - 1]], base=P, channel_multiplier=0).then_inc(const_set, 1)
            pool.iota(iota_p[:, :], pattern=[[0, 1]], base=NPAD, channel_multiplier=1).then_inc(const_set, 1)
            pool.wait_ge(const_set, 8)
            pool.affine_select(out=ident[:, :], in_=ident[:, :], compare_op=ALU.not_equal, fill=1.0,
                               base=0, pattern=[[-1, P]], channel_multiplier=1).then_inc(masks, 1)
            pool.affine_select(out=tri[:, :], in_=ones[:, :], compare_op=ALU.is_gt, fill=0.0,
                               base=0, pattern=[[1, P]], channel_multiplier=-1).then_inc(masks, 1)
            pool.affine_select(out=valid[:, :], in_=ones[:, 0:1], compare_op=ALU.is_ge, fill=0.0,
                               base=LAST - 1, pattern=[[0, 1]], channel_multiplier=-1).then_inc(masks, 1)
            pool.tensor_copy(fill[:, D:D + 1], iota_p[:, :]).then_inc(numbers, 1)
            pool.tensor_copy(xn[:, :, D], iota_n[:, :]).then_inc(numbers, 1)
            pool.tensor_copy(number_e[:, :], iota_e[:, :]).then_inc(numbers, 1)
            pool.tensor_copy(number_b[:, :], iota_b[:, :]).then_inc(numbers, 1)
            pool.memset(base[:, 0, :], 0.0).then_inc(numbers, 1)
            pool.memset(small[:, :, 3], 0.0).then_inc(numbers, 1)

            def split_low(e, p, j):
                if j % 2 == 0:
                    pool.wait_ge(high_dve, e * EVEN + (j // 2 + 1))
                else:
                    pool.wait_ge(high_act, e * ODD + (j // 2 + 1))
                pool.tensor_tensor(piece(WL[p], j), raw(j), piece(WH[p], j).bitcast(F32),
                                   ALU.subtract).then_inc(low_pool, 1)

            for j in range(1, NPC, 2):
                split_low(0, 0, j)
            for j in range(NPC):
                split_low(1, 1, j)
            pool.wait_ge(slots_ready, 1)
            pool.wait_ge(rows_filled, 16 * len(FILLS))
            for n in range(NT):
                r = LAST if n == NT - 1 else P
                for k in range(TOPK):
                    pool.indirect_dma_start(
                        out=xs[:, :], out_offset=bass.IndirectOffsetOnAxis(ap=slot_i[0:r, k, n:n + 1], axis=0),
                        in_=xn[0:r, n, :], in_offset=None).then_inc(rows_moved, 16)

            tile_no = pool.alloc_register("pool_tile")
            pool.reg_mov(tile_no, NT + 1)

            def add_rows():
                pool.wait_ge(y_taken, pool.snap(tile_no, min_val=NT + 1, max_val=NT + MAX_ROUTED))
                pool.reg_add(tile_no, tile_no, 1)
                pool.indirect_dma_start(
                    out=sums[:, :], out_offset=bass.IndirectOffsetOnAxis(ap=dest[:, 0:1], axis=0),
                    in_=ysb[:, :], in_offset=None, compute_op=ALU.add).then_inc(rows_moved, 16)

            def expert(e, p):
                n = pool.value_load(ntile_i[0:1, bass.ds(e - 1, 1)], min_val=1, max_val=MAXB)
                if p is not None:
                    for j in range(EVEN):
                        split_low(e + 1, p, j)
                add_rows()
                if p is not None:
                    for j in range(EVEN, NPC):
                        split_low(e + 1, p, j)
                with pool.If(n > 1):
                    with pool.Fori(1, n):
                        add_rows()
                with pool.Else():
                    pass

            with pool.Fori(0, (NE - 2) // 2) as q:
                expert(q * 2 + 1, 0)
                expert(q * 2 + 2, 1)
            expert(NEXP - 2, 0)
            expert(NEXP - 1, None)

        @block.scalar
        def _(act):
            act.wait_ge(par_in, 16 * 6)
            act.activation(cwh[:, :, :], cw[:, :, :], ACT.Copy).then_inc(cwh_ready, 1)
            act.wait_ge(var_ready, 1)
            act.activation(rstd[:, :], rstd[:, :], ACT.Sqrt).then_inc(std_ready, 1)
            for n in range(NT):
                act.wait_ge(xnT_psum, n + 1)
                act.activation(xnTh[:, :, n * P:(n + 1) * P],
                               ps[n % 2][:, 0:KD * P].rearrange("p (k t) -> p k t", k=KD),
                               ACT.Copy).then_inc(xnTh_ready, 1)
            def take_srow(b):
                c, w = b * 512, min(512, NPAD - b * 512)
                act.wait_ge(srow_psum, cdiv(c + w, P))
                act.activation(srow[:, c:c + w], ps[b][:, 0:w], ACT.Copy).then_inc(srow_ready, 1)

            for n in range(NT):
                act.wait_ge(node_psum, n + 1)
                act.activation(node[:, n, 0:D], ps[3 + n % 2][:, 0:D], ACT.Copy)
                act.activation(node[:, n, D + 1:2 * D + 1], ps[3 + n % 2][:, D:2 * D], ACT.Copy).then_inc(node_act, 1)
                if n >= 5 and n % 4 == 1:
                    take_srow(n // 4 - 1)
            take_srow(2)
            act.wait_ge(srow_ready, 3)
            act.wait_ge(node_dve, NT)

            def score(n):
                act.activation(e_sb[:, n, :], srow[:, :], ACT.Identity, bias=scol[:, n, 3:4]).then_inc(score_v, 1)

            score(0)
            for n in range(NT):
                if n + 1 < NT:
                    score(n + 1)
                act.wait_ge(score_w, n + 1)
                act.activation(e_sb[:, n, :], e_sb[:, n, :], ACT.Exp, scale=-1.0).then_inc(score_e, 1)
                act.wait_ge(xb_psum, n + 1)
                act.activation(xb[:, n, :], ps[3 + n % 2][:, 0:D + 2], ACT.Copy).then_inc(xb_ready, 1)
            act.wait_ge(att_sum, 1)
            act.activation(att[:, :, :], att[:, :, :], ACT.Sigmoid).then_inc(att_ready, 1)
            for n in range(NT):
                act.wait_ge(z_ready, n + 1)
                act.activation(z[:, n % 2, :], z[:, n % 2, :], ACT.Sigmoid).then_inc(gn_ready, 1)
                if n in (HALF - 1, NT - 1):
                    part = slice(0, HALF) if n < HALF else slice(HALF, NT)
                    act.wait_ge(var_ready, 2 if n < HALF else 3)
                    act.activation(rstd[:, part], rstd[:, part], ACT.Sqrt).then_inc(std_ready, 1)

            def split_high(e, p, j):
                stage_wait(act, e, j)
                act.activation(piece(WH[p], j), raw(j), ACT.Copy).then_inc(high_act, 1)

            def load_own(g):
                act.dma_start(xg[:, 0:D], xn[:, bass.ds(g, 1), 0:D].rearrange("p n d -> p (n d)"))\
                    .then_inc(x_loaded, 16)

            def load_rows(g):
                act.dma_start(xg[:, :], xs[bass.ds((g - NT) * P, P), :]).then_inc(x_loaded, 16)

            def take_xT(g):
                act.wait_ge(xT_psum, g + 1)
                act.activation(xTh[:, :, :], ps[X_BANK][:, 0:KD * P].rearrange("p (k t) -> p k t", k=KD),
                               ACT.Copy).then_inc(xTh_ready, 1)

            def tile(g, first, routed, prep, load):
                def silu(i):
                    act.wait_ge(up_done, g * NG + (i + 1))
                    if not first:
                        act.wait_ge(hT_psum, g * NG + (i + 1 - NG))
                    act.activation(hid[:, i, 0:UPS[i][1]], ps[A_BANK[i]][:, 0:UPS[i][1]], ACT.Silu)\
                        .then_inc(silu_done, 1)

                def high(i):
                    act.wait_ge(hT_psum, g * NG + (i + 1))
                    if i == 2:
                        act.wait_ge(down_done, g * NG + 1)
                    elif not first:
                        act.wait_ge(down_done, g * NG)
                    w = CHUNKS[i] * P
                    act.activation(hh[:, i % 2, 0:w], ps[H_BANK[i]][:, 0:w], ACT.Copy).then_inc(hh_ready, 1)

                def prepare(j):
                    if prep is not None:
                        split_high(prep[0], prep[1], j)

                silu(0)
                prepare(1)
                silu(1)
                high(0)
                prepare(3)
                silu(2)
                high(1)
                high(2)
                take_xT(g + 1)
                act.wait_ge(xT_ready, g + 2)
                if load is not None:
                    load(g + 2)
                act.wait_ge(down_done, g * NG + NG)
                if routed:
                    act.wait_ge(meta_ready, g + 1 - NT)
                    act.wait_ge(rows_moved, g * 16 + 16 * (SCATTERS - NT))
                    act.activation(ysb[:, :], ps[Y_BANK][:, 0:D], ACT.Copy, scale=wcol[:, 0:1]).then_inc(y_taken, 1)
                else:
                    act.wait_ge(y_taken, g + 1)
                    act.dma_start(sums[bass.ds(g * P, P), :], ysb[:, :]).then_inc(y_stored, 16)
                prepare(5)
                prepare(7)

            act.wait_ge(graph_free, 1)
            act.wait_ge(gshift, 1)
            act.activation(top[:, :, 0:TOPK], top[:, :, 0:TOPK], ACT.Exp).then_inc(gexp_ready, 1)
            for j in range(1, NPC, 2):
                split_high(0, 0, j)
            take_xT(0)
            load_own(1)
            tile(0, True, False, (1, 1), load_own)
            with act.Fori(1, NT - 2) as g:
                tile(g, False, False, None, load_own)
            act.wait_ge(rows_moved, 16 * SCATTERS)
            with act.Fori(NT - 2, NT) as g:
                tile(g, False, False, None, load_rows)
            act.wait_ge(counts_ready, 1)
            act.wait_ge(y_stored, 16 * (NT + 1))
            tile_no = act.alloc_register("act_tile")
            act.reg_mov(tile_no, NT)

            def routed_tile(prep):
                tile(act.snap(tile_no, min_val=NT, max_val=NT + MAX_ROUTED - 1), False, True, prep, load_rows)
                act.reg_add(tile_no, tile_no, 1)

            def expert(e, nxt):
                n = act.value_load(ntile_i[0:1, bass.ds(e - 1, 1)], min_val=1, max_val=MAXB)
                routed_tile(nxt)
                with act.If(n > 1):
                    with act.Fori(1, n):
                        routed_tile(None)
                with act.Else():
                    pass

            with act.Fori(0, (NE - 2) // 2) as q:
                expert(q * 2 + 1, (q * 2 + 2, 0))
                expert(q * 2 + 2, (q * 2 + 3, 1))
            expert(NEXP - 2, (NEXP - 1, 0))
            expert(NEXP - 1, None)

        @block.vector
        def _(dve):
            steps = [0]

            def link(ins):
                steps[0] += 1
                ins.then_inc(dve_step, 1)
                dve.wait_ge(dve_step, steps[0])

            dve.wait_ge(x_in, 16)
            for n in range(NT):
                last = dve.bn_stats(stats[:, n, :], xres[:, n, :])
            link(last)
            for n in range(NT):
                last = dve.bn_aggr(mv[:, n, :], stats[:, n, :])
            link(last)
            dve.tensor_scalar(rstd[:, :], mv[:, :, 1], EPS, None, ALU.add).then_inc(var_ready, 1)
            dve.wait_ge(cwh_ready, 1)
            dve.tensor_tensor(cwl[:, :, :], cw[:, :, :], cwh[:, :, :].bitcast(F32), ALU.subtract).then_inc(cw_ready, 1)
            dve.wait_ge(std_ready, 1)
            link(dve.reciprocal(rstd[:, :], rstd[:, :]))
            for n in range(NT):
                dve.tensor_scalar(xn[:, n, 0:D], xres[:, n, :], mv[:, n, 0:1], rstd[:, n:n + 1],
                                  ALU.subtract, ALU.mult).then_inc(xn1_ready, 1)
            dve.memset(node[:, :, D:D + 1], 1.0)
            dve.wait_ge(u_psum, 1)
            dve.tensor_copy(cv[:, :, 4:6], ps[2][:, 0:2 * KD].rearrange("p (k c) -> p k c", k=KD)).then_inc(u_ready, 1)
            for n in range(NT):
                dve.wait_ge(xnTh_ready, n + 1)
                cols = slice(n * P, (n + 1) * P)
                dve.tensor_tensor(xnTl[:, :, cols], ps[n % 2][:, 0:KD * P].rearrange("p (k t) -> p k t", k=KD),
                                  xnTh[:, :, cols].bitcast(F32), ALU.subtract).then_inc(xnT_ready, 1)
            for n in range(NT):
                dve.wait_ge(node_psum, n + 1)
                dve.tensor_copy(node[:, n, 2 * D + 1:CC], ps[5 + n % 2][:, 0:2])
                dve.tensor_copy(scol[:, n, :], ps[5 + n % 2][:, 2:6]).then_inc(node_dve, 1)
                dve.wait_ge(node_dve, n + 1)
                if n >= 2:
                    dve.wait_ge(srow_psum, n - 1)
                dve.tensor_copy(srep[:, n % 2, :], scol[:, n, 2:3].to_broadcast([P, P])).then_inc(srep_ready, 1)
            dve.wait_ge(adj_in, 16)

            def mask(n):
                dve.wait_ge(score_e, n + 1)
                dve.scalar_tensor_tensor(out=e_sb[:, n, :], in0=adj_sb[:, n, :], scalar=0.0, in1=e_sb[:, n, :],
                                         op0=ALU.not_equal, op1=ALU.mult).then_inc(e_ready, 1)

            for n in range(NT):
                dve.wait_ge(score_v, n + 1)
                dve.scalar_tensor_tensor(out=e_sb[:, n, :], in0=e_sb[:, n, :], scalar=0.01, in1=e_sb[:, n, :],
                                         op0=ALU.mult, op1=ALU.max).then_inc(score_w, 1)
                if n:
                    mask(n - 1)
            mask(NT - 1)
            dve.wait_ge(xb_ready, NT)
            dve.wait_ge(late_in, 48)
            link(dve.tensor_tensor(att[:, :, :], xb[:, :, D:D + 2], scol[:, :, 0:2], ALU.add))
            dve.tensor_tensor(att[:, :, :], att[:, :, :], abias[:, :].unsqueeze(1).to_broadcast([P, NT, 2]),
                              ALU.add).then_inc(att_sum, 1)
            link(dve.tensor_tensor(xb[:, :, 0:D], xb[:, :, 0:D], gbias[:, :].unsqueeze(1).to_broadcast([P, NT, D]),
                                   ALU.add))
            dve.wait_ge(att_ready, 1)
            link(dve.tensor_tensor(xb[:, :, 0:D], xb[:, :, 0:D], att[:, :, 1:2].to_broadcast([P, NT, D]), ALU.mult))

            def mix(n):
                pa = ps[n % 3]
                dve.wait_ge(xa_psum, n + 1)
                link(dve.tensor_scalar(small[:, n, 0:1], pa[:, D:D + 1], ATTN_EPS, None, ALU.add))
                link(dve.reciprocal(small[:, n, 1:2], small[:, n, 0:1]))
                link(dve.tensor_tensor(small[:, n, 2:3], small[:, n, 1:2], att[:, n, 0:1], ALU.mult))
                dve.scalar_tensor_tensor(out=z[:, n % 2, :], in0=pa[:, 0:D], scalar=small[:, n, 2:3],
                                         in1=xb[:, n, 0:D], op0=ALU.mult, op1=ALU.add).then_inc(z_ready, 1)

            def add_graph(n):
                dve.wait_ge(gn_ready, n + 1)
                link(dve.tensor_tensor(xres[:, n, :], xres[:, n, :], z[:, n % 2, :], ALU.add))
                link(dve.bn_stats(stats[:, n, :], xres[:, n, :]))
                link(dve.bn_aggr(mv[:, n, :], stats[:, n, :]))
                last = dve.tensor_scalar(rstd[:, n:n + 1], mv[:, n, 1:2], EPS, None, ALU.add)
                if n in (HALF - 1, NT - 1):
                    last.then_inc(var_ready, 1)

            def norm(n):
                if n in (0, HALF):
                    dve.wait_ge(std_ready, 2 if n == 0 else 3)
                    part = slice(0, HALF) if n == 0 else slice(HALF, NT)
                    link(dve.reciprocal(rstd[:, part], rstd[:, part]))
                dve.tensor_scalar(xn[:, n, 0:D], xres[:, n, :], mv[:, n, 0:1], rstd[:, n:n + 1],
                                  ALU.subtract, ALU.mult).then_inc(xn2_ready, 1)

            def take_xT2(n):
                dve.wait_ge(xT2_psum, n + 1)
                dve.tensor_copy(xT2[:, n % 2, :, :], ps[3 + n % 2][:, 0:KD * P].rearrange("p (k t) -> p k t", k=KD))\
                    .then_inc(xT2_ready, 1)

            def route(n):
                dve.wait_ge(gate_psum, n + 1)
                dve.tensor_tensor(gates[:, n, :], ps[5 + n % 2][:, 0:NE], rbias[:, :], ALU.add).then_inc(gate_read, 1)
                dve.wait_ge(gate_read, n + 1)
                link(dve.max(top[:, n, :], gates[:, n, :]))
                link(dve.max_index(top_i[:, n, :], top[:, n, :], gates[:, n, :]))

            for i in range(max(ROUTE) + 2):
                if i < NT:
                    mix(i)
                if 1 <= i <= NT:
                    add_graph(i - 1)
                for t in ROUTE.get(i, ()):
                    norm(t)
                for t in ROUTE.get(i, ()):
                    take_xT2(t)
                for t in ROUTE.get(i - 1, ()):
                    route(t)
                if i == max(ROUTE):
                    dve.wait_ge(xT2_ready, NT)
                    dve.sem_inc(graph_free, 1)
            dve.wait_ge(numbers, 6)
            dve.wait_ge(masks, 3)
            link(dve.tensor_copy(top_f[:, :, :], top_i[:, :, 0:TOPK]))
            for k in range(TOPK):
                last = dve.tensor_tensor(onehot[:, k, :, :], number_e[:, :].unsqueeze(1).to_broadcast([P, NT, NE]),
                                         top_f[:, :, k:k + 1].to_broadcast([P, NT, NE]), ALU.is_equal)
            link(last)
            link(dve.tensor_scalar(onehot[:, :, NT - 1, :], onehot[:, :, NT - 1, :], valid[:, 0:1], None, ALU.mult))
            link(dve.tensor_tensor(pick[:, 0:2, :, :], onehot[:, 0:2, :, :], onehot[:, 2:4, :, :], ALU.add))
            dve.tensor_tensor(chosen[:, :, :], pick[:, 0, :, :], pick[:, 1, :, :], ALU.add).then_inc(chosen_ready, 1)
            dve.tensor_tensor(top_f[:, :, :], top[:, :, 0:TOPK], top[:, :, 0:1].to_broadcast([P, NT, TOPK]),
                              ALU.subtract).then_inc(gate_read, 1)
            dve.wait_ge(gate_read, NT + 1)
            dve.tensor_copy(top[:, :, 0:TOPK], top_f[:, :, :]).then_inc(gshift, 1)
            dve.wait_ge(pos_psum, 1)
            earlier, each = (ps[b][:, 0:NT * NE].rearrange("p (n e) -> p n e", n=NT) for b in (7, 2))
            for n in range(NT):
                link(dve.tensor_tensor(base[:, n + 1, :], base[:, n, :], each[:, n, :], ALU.add))
            link(dve.tensor_tensor(above[:, :, :], base[:, NT, :].unsqueeze(2).to_broadcast([P, NE, MAXB - 1]),
                                   number_b[:, :].unsqueeze(1).to_broadcast([P, NE, MAXB - 1]), ALU.is_gt))
            link(dve.tensor_reduce(slot0[:, :], above[:, :, :], AX.X, ALU.add))
            link(dve.tensor_scalar(ntile[:, :], slot0[:, :], 1.0, None, ALU.add))
            link(dve.tensor_tensor_scan(tiles_to[:, :], ones_e[:, :], ntile[:, :], 0.0, ALU.mult, ALU.add))
            link(dve.tensor_scalar(total_f[:, :], tiles_to[:, NE - 1:NE], float(NT), None, ALU.add))
            dve.tensor_copy(ntile_i[:, :], ntile[0:1, :])
            dve.tensor_copy(total_i[:, :], total_f[0:1, :]).then_inc(counts_ready, 1)
            link(dve.tensor_tensor(slot0[:, :], tiles_to[:, :], ntile[:, :], ALU.subtract))
            link(dve.tensor_scalar(slot0[:, :], slot0[:, :], float(P), None, ALU.mult))
            link(dve.tensor_tensor(slot[:, :, :], earlier, base[:, 0:NT, :], ALU.add))
            link(dve.tensor_tensor(slot[:, :, :], slot[:, :, :], slot0[:, :].unsqueeze(1).to_broadcast([P, NT, NE]),
                                   ALU.add))
            link(dve.tensor_tensor(pick[:, :, :, :], onehot[:, :, :, :],
                                   slot[:, :, :].unsqueeze(1).to_broadcast([P, TOPK, NT, NE]), ALU.mult))
            link(dve.tensor_reduce(slot_k[:, :, :], pick[:, :, :, :], AX.X, ALU.add))
            link(dve.tensor_copy(slot_i[:, :, :], slot_k[:, :, :]))
            dve.wait_ge(gexp_ready, 1)
            link(dve.tensor_reduce(gsum[:, :], top[:, :, 0:TOPK], AX.X, ALU.add))
            link(dve.reciprocal(gsum[:, :], gsum[:, :]))
            link(dve.tensor_tensor(top_f[:, :, :], top[:, :, 0:TOPK], gsum[:, :].unsqueeze(2).to_broadcast([P, NT, TOPK]),
                                   ALU.mult))
            for k in range(TOPK):
                last = dve.tensor_tensor(pick[:, k, :, :], onehot[:, k, :, :],
                                         top_f[:, :, k:k + 1].to_broadcast([P, NT, NE]), ALU.mult)
            link(last)
            link(dve.tensor_tensor(pick[:, 0:2, :, :], pick[:, 0:2, :, :], pick[:, 2:4, :, :], ALU.add))
            dve.tensor_tensor(xn[:, :, D + 1:PW], pick[:, 0, :, :], pick[:, 1, :, :], ALU.add).then_inc(slots_ready, 1)

            def split_high(e, p, j):
                stage_wait(dve, e, j)
                dve.tensor_copy(piece(WH[p], j), raw(j)).then_inc(high_dve, 1)

            def take_xT(g, routed):
                dve.wait_ge(xTh_ready, g + 1)
                if routed:
                    dve.tensor_copy(meta[:, :], xg[:, D:PW]).then_inc(meta_read, 1)
                dve.tensor_tensor(xTl[:, :, :], ps[X_BANK][:, 0:KD * P].rearrange("p (k t) -> p k t", k=KD),
                                  xTh[:, :, :].bitcast(F32), ALU.subtract).then_inc(xT_ready, 1)

            def tile(g, e, prep, next_routed, first=False):
                def times(i):
                    w = UPS[i][1]
                    dve.wait_ge(silu_done, g * NG + (i + 1))
                    dve.tensor_tensor(hid[:, i, 0:w], hid[:, i, 0:w], ps[B_BANK[i]][:, 0:w], ALU.mult)\
                        .then_inc(h_done, 1)

                def low(i):
                    w = CHUNKS[i] * P
                    dve.wait_ge(hh_ready, g * NG + (i + 1))
                    dve.tensor_tensor(hl[:, i % 2, 0:w], ps[H_BANK[i]][:, 0:w], hh[:, i % 2, 0:w].bitcast(F32),
                                      ALU.subtract).then_inc(hl_ready, 1)

                def prepare(j):
                    if prep is not None:
                        split_high(prep[0], prep[1], j)

                times(0)
                prepare(0)
                prepare(2)
                times(1)
                low(0)
                prepare(4)
                if e is not None:
                    dve.wait_ge(meta_read, g + 1 - NT)
                    dve.wait_ge(rows_moved, g * 16 + 16 * (SCATTERS - NT))
                    dve.tensor_copy(dest[:, :], meta[:, 0:1])
                    dve.tensor_copy(wcol[:, :], meta[:, bass.ds(e, 1)]).then_inc(meta_ready, 1)
                times(2)
                low(1)
                low(2)
                take_xT(g + 1, next_routed)
                if e is None:
                    dve.wait_ge(down_done, g * NG + NG)
                    dve.wait_ge(y_stored, g * 16 + 16)
                    own = xres[:, bass.ds(g, 1), :].rearrange("p n d -> p (n d)")
                    dve.tensor_tensor(ysb[:, :], ps[Y_BANK][:, 0:D], own, ALU.add).then_inc(y_taken, 1)
                prepare(6)
                prepare(8)

            for j in range(0, NPC, 2):
                split_high(0, 0, j)
                dve.wait_ge(high_dve, j // 2 + 1)
                dve.tensor_tensor(piece(WL[0], j), raw(j), piece(WH[0], j).bitcast(F32), ALU.subtract)\
                    .then_inc(low_dve, 1)
            dve.memset(hid[:, NG - 1, UPS[-1][1]:CHUNKS[-1] * P], 0.0)
            take_xT(0, False)
            tile(0, None, (1, 1), False, True)
            with dve.Fori(1, NT - 1) as g:
                tile(g, None, None, False)
            tile(NT - 1, None, None, True)
            tile_no = dve.alloc_register("dve_tile")
            dve.reg_mov(tile_no, NT)

            def routed_tile(e, prep):
                tile(dve.snap(tile_no, min_val=NT, max_val=NT + MAX_ROUTED - 1), e, prep, True)
                dve.reg_add(tile_no, tile_no, 1)

            def expert(e, nxt):
                n = dve.value_load(ntile_i[0:1, bass.ds(e - 1, 1)], min_val=1, max_val=MAXB)
                routed_tile(e, nxt)
                with dve.If(n > 1):
                    with dve.Fori(1, n):
                        routed_tile(e, None)
                with dve.Else():
                    pass

            dve.wait_ge(counts_ready, 1)
            with dve.Fori(0, (NE - 2) // 2) as q:
                expert(q * 2 + 1, (q * 2 + 2, 0))
                expert(q * 2 + 2, (q * 2 + 3, 1))
            expert(NEXP - 2, (NEXP - 1, 0))
            expert(NEXP - 1, None)

        @block.tensor
        def _(pe):
            pe.wait_ge(masks, 1)
            pe.wait_ge(par_in, 16 * 6)
            for c in range(KD):
                for k in range(KD):
                    last = pe.matmul(ps[2][:, 2 * c:2 * c + 2], wsT[:, k, c * P:(c + 1) * P], ac[:, k, :],
                                     start=(k == 0), stop=(k == KD - 1))
            last.then_inc(u_psum, 1)

            def transpose_xn(n):
                pe.wait_ge(xn1_ready, n + 1)
                if n >= 2:
                    pe.wait_ge(xnT_ready, n - 1)
                for k in range(KD):
                    last = pe.transpose(ps[n % 2][:, k * P:(k + 1) * P], xn[:, n, k * P:(k + 1) * P], ident[:, :])
                last.then_inc(xnT_psum, 1)

            def node_row(n):
                cols = slice(n * P, (n + 1) * P)
                pe.wait_ge(xnT_ready, n + 1)
                if n >= 2:
                    pe.wait_ge(node_act, n - 1)
                    pe.wait_ge(node_dve, n - 1)
                for k in range(KD):
                    for m, (a, w) in enumerate(((xnTh, cwh), (xnTl, cwh), (xnTh, cwl))):
                        pe.matmul(ps[3 + n % 2][:, :], a[:, k, cols], w[:, k, :],
                                  start=(k == 0 and m == 0), stop=(k == KD - 1 and m == 2))
                for k in range(KD):
                    for m, a in enumerate((xnTh, xnTl)):
                        last = pe.matmul(ps[5 + n % 2][:, 0:6], a[:, k, cols].bitcast(F32), cv[:, k, :],
                                         start=(k == 0 and m == 0), stop=(k == KD - 1 and m == 1))
                last.then_inc(node_psum, 1)

            def left_row(n):
                pe.wait_ge(srep_ready, n + 1)
                pe.matmul(ps[n // 4][:, n % 4 * P:(n % 4 + 1) * P], srep[:, n % 2, :], ident[:, :],
                          start=True, stop=True).then_inc(srow_psum, 1)

            for n in range(NT):
                transpose_xn(n)
            pe.wait_ge(u_ready, 1)
            pe.wait_ge(cw_ready, 1)
            for n in range(NT):
                node_row(n)
                if n:
                    left_row(n - 1)
            left_row(NT - 1)
            pe.wait_ge(adj_in, 16)
            pe.wait_ge(node_act, NT)
            pe.wait_ge(node_dve, NT)
            for i in range(NT):
                if i >= 2:
                    pe.wait_ge(xb_ready, i - 1)
                for n in range(NT):
                    last = pe.matmul(ps[3 + i % 2][:, 0:D + 2], adj_sb[:, n, i * P:(i + 1) * P], node[:, n, D + 1:CC],
                                     start=(n == 0), stop=(n == NT - 1))
                last.then_inc(xb_psum, 1)
            for i in range(max(ROUTE) + 2):
                if i < NT:
                    if i == 0:
                        pe.wait_ge(srow_ready, 3)
                    if i >= 3:
                        pe.wait_ge(z_ready, i - 2)
                    for n in range(NT):
                        if i == 0:
                            pe.wait_ge(e_ready, n + 1)
                        last = pe.matmul(ps[i % 3][:, 0:D + 1], e_sb[:, n, i * P:(i + 1) * P], node[:, n, 0:D + 1],
                                         start=(n == 0), stop=(n == NT - 1))
                    last.then_inc(xa_psum, 1)
                for t in ROUTE.get(i - 1, ()):
                    pe.wait_ge(xT2_ready, t + 1)
                    if t >= 2:
                        pe.wait_ge(gate_read, t - 1)
                    for k in range(KD):
                        last = pe.matmul(ps[5 + t % 2][:, 0:NE], xT2[:, t % 2, k, :], gatew[:, k, :],
                                         start=(k == 0), stop=(k == KD - 1))
                    last.then_inc(gate_psum, 1)
                for t in ROUTE.get(i, ()):
                    pe.wait_ge(xn2_ready, t + 1)
                    if t >= 2:
                        pe.wait_ge(xT2_ready, t - 1)
                    if t == 0:
                        pe.wait_ge(xb_ready, NT)
                    for k in range(KD):
                        last = pe.transpose(ps[3 + t % 2][:, k * P:(k + 1) * P], xn[:, t, k * P:(k + 1) * P], ident[:, :])
                    last.then_inc(xT2_psum, 1)
            pe.wait_ge(gate_read, NT)
            for k in range(KD):
                last = pe.transpose(ps[X_BANK][:, k * P:(k + 1) * P], xn[:, 0, k * P:(k + 1) * P], ident[:, :])
            last.then_inc(xT_psum, 1)
            pe.wait_ge(masks, 3)
            pe.wait_ge(chosen_ready, 1)
            picked = chosen[:, :, :].rearrange("p n e -> p (n e)")
            pe.matmul(ps[7][:, 0:NT * NE], tri[:, :], picked, start=True, stop=True)
            pe.matmul(ps[2][:, 0:NT * NE], ones[:, :], picked, start=True, stop=True).then_inc(pos_psum, 1)

            def transpose_x(g):
                pe.wait_ge(x_loaded, g * 16)
                for k in range(KD):
                    last = pe.transpose(ps[X_BANK][:, k * P:(k + 1) * P], xg[:, k * P:(k + 1) * P], ident[:, :])
                last.then_inc(xT_psum, 1)

            def up(p, i):
                w = UPS[i][1]
                for m, bank in enumerate((A_BANK[i], B_BANK[i])):
                    for k in range(KD):
                        o = AT[KD * i + k] + m * w
                        for s, (a, b) in enumerate(((xTh, WH), (xTl, WH), (xTh, WL))):
                            last = pe.matmul(ps[bank][:, 0:w], a[:, k, :], b[p][:, o:o + w],
                                             start=(k == 0 and s == 0), stop=(k == KD - 1 and s == 2))
                last.then_inc(up_done, 1)

            def transpose_h(i):
                for c in range(CHUNKS[i]):
                    last = pe.transpose(ps[H_BANK[i]][:, c * P:(c + 1) * P], hid[:, i, c * P:(c + 1) * P], ident[:, :])
                last.then_inc(hT_psum, 1)

            def down(p, i):
                for c in range(CHUNKS[i]):
                    cols, o = slice(c * P, (c + 1) * P), AT[KD * NG + i] + c * D
                    for s, (a, b) in enumerate(((hh, WH), (hh, WL), (hl, WH))):
                        last = pe.matmul(ps[Y_BANK][:, 0:D], a[:, i % 2, cols], b[p][:, o:o + D],
                                         start=(i == 0 and c == 0 and s == 0),
                                         stop=(i == NG - 1 and c == CHUNKS[i] - 1 and s == 2))
                last.then_inc(down_done, 1)

            def tile(g, p, first, e):
                def weights(*pieces):
                    if e is not None:
                        for j in pieces:
                            low_wait(pe, e, j)

                pe.wait_ge(xT_ready, g + 1)
                if not first:
                    pe.wait_ge(h_done, g * NG)
                    pe.wait_ge(hl_ready, g * NG)
                weights(0, 1)
                up(p, 0)
                weights(2, 3)
                up(p, 1)
                pe.wait_ge(h_done, g * NG + 1)
                transpose_h(0)
                weights(4, 5)
                up(p, 2)
                pe.wait_ge(h_done, g * NG + 2)
                transpose_h(1)
                pe.wait_ge(hl_ready, g * NG + 1)
                if not first:
                    pe.wait_ge(y_taken, g)
                weights(6)
                down(p, 0)
                pe.wait_ge(h_done, g * NG + 3)
                transpose_h(2)
                transpose_x(g + 1)
                pe.wait_ge(hl_ready, g * NG + 2)
                weights(7)
                down(p, 1)
                pe.wait_ge(hl_ready, g * NG + 3)
                weights(8)
                down(p, 2)

            tile(0, 0, True, 0)
            with pe.Fori(1, NT) as g:
                tile(g, 0, False, None)
            tile_no = pe.alloc_register("pe_tile")
            pe.reg_mov(tile_no, NT)

            def routed_tile(p, e):
                tile(pe.snap(tile_no, min_val=NT, max_val=NT + MAX_ROUTED - 1), p, False, e)
                pe.reg_add(tile_no, tile_no, 1)

            def expert(e, p):
                n = pe.value_load(ntile_i[0:1, bass.ds(e - 1, 1)], min_val=1, max_val=MAXB)
                routed_tile(p, e)
                with pe.If(n > 1):
                    with pe.Fori(1, n):
                        routed_tile(p, None)
                with pe.Else():
                    pass

            pe.wait_ge(counts_ready, 1)
            with pe.Fori(0, (NE - 2) // 2) as q:
                expert(q * 2 + 1, 1)
                expert(q * 2 + 2, 0)
            expert(NEXP - 2, 1)
            expert(NEXP - 1, 0)


def _layout(inputs):
    import numpy as np

    a = {k: np.asarray(v) for k, v in inputs.items()}
    n, d = a["x"].shape
    pad = cdiv(n, P) * P
    x = np.zeros((pad, d), a["x"].dtype)
    x[:n] = a["x"]
    adj = np.zeros((pad, pad), a["adj"].dtype)
    adj[:n, :n] = a["adj"].T
    wa, wb, a_sa = a["L0_gnn_Wa"], a["L0_gnn_Wb"], a["L0_gnn_a_sa"]
    w1 = np.concatenate([a["L0_ffn_sw1"][None], a["L0_ffn_w1"]])
    w2 = np.concatenate([a["L0_ffn_sw2"][None], a["L0_ffn_w2"]])
    w3 = np.concatenate([a["L0_ffn_sw3"][None], a["L0_ffn_w3"]])
    ne, _, h = w1.shape
    groups = up_groups(h)
    hw = sum(w for _, w in groups)
    hc = cdiv(hw, P)

    def wide(w, axis, n):
        widths = [(0, 0)] * 3
        widths[axis] = (0, n - h)
        return np.pad(w, widths)

    ups = [wide(w, 2, hw).reshape(ne, d // P, P, hw) for w in (w1, w2)]
    down = wide(w3, 1, hc * P).reshape(ne, hc, P, d)
    parts = [u[:, k, :, c:c + w] for c, w in groups for k in range(d // P) for u in ups]
    parts += [down[:, c] for c in range(hc)]
    return {
        "x": x,
        "adjT": adj,
        "w_sa": a["L0_gnn_W_sa"],
        "w_saT": a["L0_gnn_W_sa"].T,
        "w_gcn": a["L0_gnn_W_gcnb"],
        "a_cols": a_sa.reshape(2, d).T,
        "attn_cols": np.stack([wa[0, :d], wb[0, :d], wa[0, d:], wb[0, d:]], axis=1),
        "attn_bias": np.concatenate([a["L0_gnn_ba"], a["L0_gnn_bb"]]),
        "gcn_bias": a["L0_gnn_b_gcnb"],
        "gate_w": a["L0_ffn_gate_w"],
        "routing_bias": a["L0_ffn_routing_bias"],
        "w_ffn": np.concatenate(parts, axis=2),
    }


def kernel(**inputs):
    import numpy as np
    import concourse.bacc as bacc
    from concourse.bass_utils import run_bass_kernel_spmd

    shape = np.asarray(inputs["x"]).shape
    nc = bacc.Bacc("TRN2", target_bir_lowering=False, num_devices=1)
    arrays, args = {}, []
    for name, a in _layout(inputs).items():
        arrays[f"in_{name}"] = np.ascontiguousarray(a)
        args.append(nc.dram_tensor(f"in_{name}", a.shape, mybir.dt.from_np(a.dtype), kind="ExternalInput").ap())
    out = nc.dram_tensor("out", shape, F32, kind="ExternalOutput").ap()
    hidden = np.asarray(inputs["L0_ffn_sw1"]).shape[1]
    graph_attention_and_routed_experts(nc, *args, hidden, out)
    r = run_bass_kernel_spmd(nc, [arrays], core_ids=[0])
    return r.results[0]["out"]
```

```python
from contextlib import ExitStack

import concourse.bass as bass
from concourse import mybir

F32 = mybir.dt.float32
F32R = mybir.dt.float32r
U32 = mybir.dt.uint32
I32 = mybir.dt.int32
ALU = mybir.AluOpType
ACT = mybir.ActivationFunctionType
AX = mybir.AxisListType

P = 128
EPS = 1e-5
ATTN_EPS = 1e-5
TOPK = 4


def cdiv(a, b):
    return -(-a // b)


def hidden_chunks(hidden):
    return [min(P, cdiv(hidden, 8) * 8 - c) for c in range(0, hidden, P)]


def graph_attention_and_routed_experts(nc, x, adjT, w_sa, w_saT, w_gcn, a_cols, attn_cols,
                                       attn_bias, gcn_bias, gate_w, routing_bias, w_ffn, hidden, out):
    NTOK, D = out.shape
    NT = x.shape[0] // P
    NPAD = NT * P
    LAST = NTOK - (NT - 1) * P
    KD = D // P
    NE = gate_w.shape[1]
    NEXP = NE + 1
    CHUNKS = hidden_chunks(hidden)
    NC = len(CHUNKS)
    PIECES = [2 * KD * w + D for w in CHUNKS]
    WCOLS = sum(PIECES)
    AT = [sum(PIECES[:j]) for j in range(NC)]
    LOW_DVE = list(range(0, NC, 4))
    LOW_POOL = [j for j in range(NC) if j % 4]
    EVEN, ODD = (NC + 1) // 2, NC // 2
    WIDE = 3
    SHARED = [WIDE] * (NT // WIDE) + ([NT % WIDE] if NT % WIDE else [])
    NSH = len(SHARED)
    BLOCK = WIDE * P
    NARROW = BLOCK - P // 2
    DIGIT = 5
    PER_WORD = 24 // DIGIT
    WORDS = cdiv(NE, PER_WORD)
    LAG = 2
    MAX_ROUTED = TOPK * NTOK // P + 2 * NE
    XS_TILES = MAX_ROUTED + WIDE
    MAXB = NT
    PW = D + 1 + NE
    STAGE = 4
    GROUPS = [(0, 6), (6, 9), (9, NT)]
    GROUP_ENDS = [b - 1 for _, b in GROUPS]
    ROUTE = {7: (0, 1), 8: (2, 3), 9: (4, 5)}
    MID, LATE = (tuple(range(*g)) for g in GROUPS[1:])

    def before(j, ring):
        return max(c for c in range(NC) if c % ring == j % ring)

    xs = nc.dram_tensor("expert_inputs", [XS_TILES * P, PW], F32, kind="Internal").ap()
    sums = nc.dram_tensor("token_sums", [NPAD + P, D], F32, kind="Internal").ap()

    with ExitStack() as ctx:
        def sem(name):
            return ctx.enter_context(nc.semaphore(name))

        def sb(name, shape, dt=F32):
            return ctx.enter_context(nc.sbuf_tensor(name, shape, dt))

        xres = sb("xres", [P, NT, D])
        xn = sb("xn", [P, NT, PW])
        ident = sb("ident", [P, P])
        tri = sb("tri", [P, P])
        ones = sb("ones", [P, P])
        valid = sb("valid", [P, 1])
        gatew = sb("gatew", [P, KD, NE])
        rbias = sb("rbias", [P, NE])
        iota_n = sb("iota_n", [P, NT], I32)
        iota_e = sb("iota_e", [P, NE], I32)
        iota_b = sb("iota_b", [P, MAXB - 2], I32)
        iota_p = sb("iota_p", [P, 1], I32)
        number_e = sb("number_e", [P, NE])
        number_b = sb("number_b", [P, MAXB - 2])
        sign_b = sb("sign_b", [P, MAXB - 2])
        odd = sb("odd", [P, NE])
        kind = sb("kind", [P, NE])
        rest = sb("rest", [P, NE])
        gap = sb("gap", [P, NE])
        upto = sb("upto", [P, NE])
        extra = sb("extra", [P, NE])
        digit = sb("digit", [P, WORDS, PER_WORD])
        place = sb("place", [P, WORDS, PER_WORD])
        words = sb("words", [P, WORDS])
        words_i = sb("words_i", [1, WORDS], I32)
        gates = sb("gates", [P, NT, NE])
        top = sb("top", [P, NT, 8])
        top_i = sb("top_i", [P, NT, 8], U32)
        top_f = sb("top_f", [P, NT, TOPK])
        onehot = sb("onehot", [P, TOPK, NT, NE])
        pick = sb("pick", [P, TOPK, NT, NE])
        chosen = sb("chosen", [P, NT, NE])
        base = sb("base", [P, NT + 1, NE])
        above = sb("above", [P, NE, MAXB - 2])
        ntile = sb("ntile", [P, NE])
        tiles_to = sb("tiles_to", [P, NE])
        slot0 = sb("slot0", [P, NE])
        ones_e = sb("ones_e", [P, NE])
        slot = sb("slot", [P, NT, NE])
        slot_k = sb("slot_k", [P, TOPK, NT])
        slot_i = sb("slot_i", [P, TOPK, NT], U32)
        total_i = sb("total_i", [1, 1], I32)
        total_f = sb("total_f", [P, 1])
        gsum = sb("gsum", [P, NT])
        stats = sb("stats", [P, NT, 6])
        mv = sb("mv", [P, NT, 2])
        rstd = sb("rstd", [P, NT])
        small = sb("small", [P, NT, 4])

        graph = ExitStack()

        def gsb(name, shape, dt=F32):
            return graph.enter_context(nc.sbuf_tensor(name, shape, dt))

        adj_sb = gsb("adj_sb", [P, NT, NPAD])
        srow = gsb("srow", [P, NPAD])
        node_adj = gsb("node_adj", [P, NT, D + 2])
        node = gsb("node", [P, NT, D + 1])
        xb = gsb("xb", [P, NT, D + 2])
        scol = gsb("scol", [P, NT, 4])
        z = gsb("z", [P, 2, D])
        xT2 = gsb("xT2", [P, 3, KD, P])
        fill = gsb("fill", [P, PW])
        abias = gsb("abias", [P, 2])
        gbias = gsb("gbias", [P, D])
        att = gsb("att", [P, NT, 2])
        rows = ExitStack()

        def rsb(name, shape, dt=F32):
            return rows.enter_context(nc.sbuf_tensor(name, shape, dt))

        xnTh = rsb("xnTh", [P, KD, NPAD], F32R)
        xnTl = rsb("xnTl", [P, KD, NPAD], F32R)
        xnT = rsb("xnT", [P, KD, NPAD])
        cw = rsb("cw", [P, KD, 2 * D])
        cwh = rsb("cwh", [P, KD, 2 * D], F32R)
        cwl = rsb("cwl", [P, KD, 2 * D], F32R)
        cv = rsb("cv", [P, KD, 6])
        wsT = rsb("wsT", [P, KD, D])
        ac = rsb("ac", [P, KD, 2])
        srep = rsb("srep", [P, 2, P])
        rows.close()
        e_sb = gsb("e_sb", [P, NT, NPAD])
        graph.close()

        experts = ExitStack()

        def esb(name, shape, dt=F32):
            return experts.enter_context(nc.sbuf_tensor(name, shape, dt))

        WH, WL = [esb("w_high0", [P, WCOLS], F32R)], [esb("w_low0", [P, WCOLS], F32R)]
        stage = [esb(f"stage{i}", [P, max(PIECES)]) for i in range(STAGE)]
        WH += [esb("w_high1", [P, WCOLS], F32R)]
        WL += [esb("w_low1", [P, WCOLS], F32R)]
        xg = esb("xg", [P, WIDE, PW])
        xTf = esb("xTf", [P, KD, BLOCK])
        xTh = esb("xTh", [P, KD, BLOCK], F32R)
        xTl = esb("xTl", [P, KD, BLOCK], F32R)
        hid = esb("hid", [P, 2, BLOCK])
        hh = esb("hh", [P, 2, BLOCK], F32R)
        hl = esb("hl", [P, 2, BLOCK], F32R)
        ysb = esb("ysb", [P, WIDE, D])
        meta = esb("meta", [P, WIDE, PW - D])
        dest = esb("dest", [P, WIDE], U32)
        wcol = esb("wcol", [P, WIDE])
        experts.close()

        ps = [ctx.enter_context(nc.psum_tensor(f"bank{i}", [P, 512], F32)) for i in range(8)]
        A_BANK, B_BANK, Y_BANK, X_BANK = (0, 2), (1, 3), (4, 5, 6), 7

        x_in = [sem(f"x_in{i}") for i in range(2)]
        par_in, adj_in, late_in = sem("par_in"), sem("adj_in"), sem("late_in")
        const_set, masks, numbers = sem("const_set"), sem("masks"), sem("numbers")
        dve_step = sem("dve_step")
        var_ready, std_ready = sem("var_ready"), sem("std_ready")
        xn1_ready, xnT_psum, xnTh_ready, xnT_ready = (
            sem("xn1_ready"), sem("xnT_psum"), sem("xnTh_ready"), sem("xnT_ready"))
        xnT_whole = sem("xnT_whole")
        u_psum, u_ready, cwh_ready, cw_ready = sem("u_psum"), sem("u_ready"), sem("cwh_ready"), sem("cw_ready")
        node_psum, node_act, node_dve = sem("node_psum"), sem("node_act"), sem("node_dve")
        srep_ready, srow_psum, srow_ready = sem("srep_ready"), sem("srow_psum"), sem("srow_ready")
        score_v, score_w, score_e, e_ready = sem("score_v"), sem("score_w"), sem("score_e"), sem("e_ready")
        xb_psum, xb_ready = sem("xb_psum"), sem("xb_ready")
        att_sum, att_ready = sem("att_sum"), sem("att_ready")
        xa_psum, z_ready, gn_ready = sem("xa_psum"), sem("z_ready"), sem("gn_ready")
        xn2_ready, xT2_psum, xT2_ready = sem("xn2_ready"), sem("xT2_psum"), sem("xT2_ready")
        gate_psum, gate_read, chosen_ready, pos_psum = (
            sem("gate_psum"), sem("gate_read"), sem("chosen_ready"), sem("pos_psum"))
        counts_ready, slots_ready = sem("counts_ready"), sem("slots_ready")
        gshift, gexp_ready = sem("gshift"), sem("gexp_ready")
        adj_free = sem("adj_free")
        rows_filled = sem("rows_filled")
        stage_in = [sem(f"stage_in{i}") for i in range(STAGE)]
        high_dve, high_act, low_dve, low_pool = sem("high_dve"), sem("high_act"), sem("low_dve"), sem("low_pool")
        x_loaded, xT_psum, xTf_ready, xTh_ready, xT_ready = (
            sem("x_loaded"), sem("xT_psum"), sem("xTf_ready"), sem("xTh_ready"), sem("xT_ready"))
        gate_done, up_done, silu_done, h_done = sem("gate_done"), sem("up_done"), sem("silu_done"), sem("h_done")
        hh_ready, hl_ready, down_done = sem("hh_ready"), sem("hl_ready"), sem("down_done")
        meta_read, meta_ready, pos_read = sem("meta_read"), sem("meta_ready"), sem("pos_read")
        y_taken, y_stored, out_stored = sem("y_taken"), sem("y_stored"), sem("out_stored")
        rows_moved = sem("rows_moved")
        SCATTERS = NT * TOPK

        FILLS = [(r, min(4, XS_TILES - r)) for r in range(0, XS_TILES, 4)]

        def norm_bank(t):
            if t in LATE:
                return X_BANK, (t - LATE[0]) * KD * P, NT
            if t in MID:
                q = t - MID[0]
                return (4, 6)[q // 2], q % 2 * KD * P, LATE[0]
            return 3 + t % 2, 0, t + 1

        def gate_bank(t):
            if t in LATE:
                return X_BANK, (t - LATE[0]) * NE, NT
            if t in MID:
                return 5, (t - MID[0]) * NE, LATE[0]
            if t in ROUTE[NT - 2]:
                return 5, (t - ROUTE[NT - 2][0]) * NE, MID[0]
            return 5 + t % 2, 0, t + 1

        def low_wait(eng, e, j):
            done, mine = (low_pool, LOW_POOL) if j % 4 else (low_dve, LOW_DVE)
            eng.wait_ge(done, e * len(mine) + (mine.index(j) + 1))

        def low_wait_before(eng, e, j):
            done, mine = (low_pool, LOW_POOL) if j % 4 else (low_dve, LOW_DVE)
            eng.wait_ge(done, (e - 1) * len(mine) + (mine.index(j) + 1))

        def high_wait(eng, e, j):
            if j % 2:
                eng.wait_ge(high_act, e * ODD + (j // 2 + 1))
            else:
                eng.wait_ge(high_dve, e * EVEN + (j // 2 + 1))

        def stage_wait(eng, e, j):
            uses = len(range(j % STAGE, NC, STAGE))
            eng.wait_ge(stage_in[j % STAGE], e * (16 * uses) + 16 * (j // STAGE + 1))

        def piece(buf, j):
            return buf[:, AT[j]:AT[j] + PIECES[j]]

        def raw(j):
            return stage[j % STAGE][:, 0:PIECES[j]]

        SPLIT_AT = {0: (0, 1), **{c: (c + 1,) for c in range(1, NC - 4)}, NC - 4: (NC - 3, NC - 2), NC - 3: (NC - 1,)}
        TAKE_X = (5, 7)
        X_PARTS = [(0, NT // 2), (NT // 2, NT)]
        TAKE_X_FIRST = (7, 9)

        def pieces_at(c, prep):
            return () if prep is None else SPLIT_AT.get(c, ())

        def load_words(eng, name):
            word = [eng.alloc_register(f"{name}_word{i}") for i in range(WORDS)]
            for i, w in enumerate(word):
                eng.reg_load(w, words_i[0:1, i:i + 1])
            regs = (word, *(eng.alloc_register(f"{name}_{what}") for what in ("kind", "more", "more_now")))
            take_digit(eng, regs)
            return regs

        def take_digit(eng, regs):
            word, kind_next, more_next, _ = regs
            whole = (1 << (DIGIT * PER_WORD)) - 1
            lowest = eng.snap(word[0], min_val=0, max_val=whole)
            eng.reg_mov(kind_next, lowest & 3)
            eng.reg_mov(more_next, (lowest >> 2) & ((1 << (DIGIT - 2)) - 1))
            for i, w in enumerate(word):
                eng.reg_alu(w, w, DIGIT, ALU.logical_shift_right)
                if i + 1 < WORDS:
                    after = eng.snap(word[i + 1], min_val=0, max_val=whole)
                    eng.reg_add(w, w, (after & ((1 << DIGIT) - 1)) << (DIGIT * (PER_WORD - 1)))

        def go_on(eng, regs):
            _, _, more_next, more_now = regs
            eng.reg_mov(more_now, more_next)
            take_digit(eng, regs)

        def first_kind(eng, regs):
            return eng.snap(regs[1], min_val=0, max_val=2)

        def blocks_more(eng, regs):
            return eng.snap(regs[3], min_val=0, max_val=MAXB // 2)

        block = ctx.enter_context(nc.Block())

        @block.sync
        def _(sp):
            for i, (a, b) in enumerate(X_PARTS):
                sp.dma_start(xres[:, a:b, :], x[a * P:b * P, :].rearrange("(n p) d -> p n d", p=P)).then_inc(x_in[i], 16)
            sp.dma_start(cw[:, :, 0:D], w_sa.rearrange("(k p) n -> p k n", p=P)).then_inc(par_in, 16)
            sp.dma_start(cw[:, :, D:2 * D], w_gcn.rearrange("(k p) n -> p k n", p=P)).then_inc(par_in, 16)
            sp.dma_start(wsT[:, :, :], w_saT.rearrange("(k p) n -> p k n", p=P)).then_inc(par_in, 16)
            sp.dma_start(ac[:, :, :], a_cols.rearrange("(k p) n -> p k n", p=P)).then_inc(par_in, 16)
            sp.dma_start(cv[:, :, 0:4], attn_cols.rearrange("(k p) n -> p k n", p=P)).then_inc(par_in, 16)
            sp.dma_start(gatew[:, :, :], gate_w.rearrange("(k p) n -> p k n", p=P)).then_inc(par_in, 16)
            sp.dma_start(adj_sb[:, :, :], adjT.rearrange("(n p) i -> p n i", p=P)).then_inc(adj_in, 16)
            sp.dma_start(gbias[:, :], gcn_bias.partition_broadcast(P)).then_inc(late_in, 16)
            sp.dma_start(abias[:, :], attn_bias.partition_broadcast(P)).then_inc(late_in, 16)
            sp.dma_start(rbias[:, :], routing_bias.partition_broadcast(P)).then_inc(late_in, 16)
            sp.wait_ge(numbers, 9 + PER_WORD)
            for r, n in FILLS:
                sp.dma_start(xs[r * P:(r + n) * P, :].rearrange("(q p) d -> p q d", p=P),
                             fill[:, :].unsqueeze(1).to_broadcast([P, n, PW])).then_inc(rows_filled, 16)
            sp.dma_start(sums[NPAD:NPAD + P, :], fill[:, 0:D]).then_inc(y_stored, 16)
            sp.wait_ge(rows_filled, 16 * len(FILLS))
            sp.wait_ge(y_stored, 16)
            sp.wait_ge(adj_free, 1)

            def load_expert(e):
                for j in range(NC):
                    if j >= STAGE:
                        low_wait(sp, e, j - STAGE)
                    elif not (isinstance(e, int) and e == 0):
                        low_wait_before(sp, e, before(j, STAGE))
                    src = w_ffn[e, :, AT[j]:AT[j] + PIECES[j]] if isinstance(e, int) else \
                        w_ffn[bass.ds(e, 1), :, AT[j]:AT[j] + PIECES[j]].rearrange("e p n -> (e p) n")
                    sp.dma_start(raw(j), src).then_inc(stage_in[j % STAGE], 16)

            load_expert(0)
            load_expert(1)
            with sp.Fori(2, NEXP) as e:
                load_expert(e)
            sp.wait_ge(counts_ready, 1)
            total = sp.value_load(total_i[0:1, 0:1], min_val=NT + NE, max_val=NT + MAX_ROUTED)
            all_added = sp.alloc_register("all_added")
            sp.reg_mov(all_added, total * 16 + 16 * (SCATTERS - NT))
            sp.wait_ge(rows_moved, all_added)
            flat = "t d -> (t d)"
            sp.dma_start(out.rearrange(flat).rearrange("(a b) -> a b", a=16),
                         sums[0:NTOK, :].rearrange(flat).rearrange("(a b) -> a b", a=16)).then_inc(out_stored, 16)
            sp.wait_ge(out_stored, 16)

        @block.gpsimd
        def _(pool):
            pool.memset(ident[:, :], 0.0).then_inc(const_set, 1)
            pool.memset(ones[:, :], 1.0).then_inc(const_set, 1)
            pool.memset(fill[:, :], 0.0).then_inc(const_set, 1)
            pool.memset(ones_e[:, :], 1.0).then_inc(const_set, 1)
            pool.iota(iota_n[:, :], pattern=[[P, NT]], base=0, channel_multiplier=1).then_inc(const_set, 1)
            pool.iota(iota_e[:, :], pattern=[[1, NE]], base=0, channel_multiplier=0).then_inc(const_set, 1)
            pool.iota(iota_b[:, :], pattern=[[P, MAXB - 2]], base=2 * P, channel_multiplier=0).then_inc(const_set, 1)
            pool.iota(iota_p[:, :], pattern=[[0, 1]], base=NPAD, channel_multiplier=1).then_inc(const_set, 1)
            pool.wait_ge(const_set, 8)
            pool.affine_select(out=ident[:, :], in_=ident[:, :], compare_op=ALU.not_equal, fill=1.0,
                               base=0, pattern=[[-1, P]], channel_multiplier=1).then_inc(masks, 1)
            pool.affine_select(out=tri[:, :], in_=ones[:, :], compare_op=ALU.is_gt, fill=0.0,
                               base=0, pattern=[[1, P]], channel_multiplier=-1).then_inc(masks, 1)
            pool.affine_select(out=valid[:, :], in_=ones[:, 0:1], compare_op=ALU.is_ge, fill=0.0,
                               base=LAST - 1, pattern=[[0, 1]], channel_multiplier=-1).then_inc(masks, 1)
            pool.tensor_copy(fill[:, D:D + 1], iota_p[:, :]).then_inc(numbers, 1)
            pool.tensor_copy(xn[:, :, D], iota_n[:, :]).then_inc(numbers, 1)
            pool.tensor_copy(number_e[:, :], iota_e[:, :]).then_inc(numbers, 1)
            pool.tensor_copy(number_b[:, :], iota_b[:, :]).then_inc(numbers, 1)
            pool.memset(base[:, 0, :], 0.0).then_inc(numbers, 1)
            pool.memset(small[:, :, 3], 0.0).then_inc(numbers, 1)
            pool.memset(digit[:, :, :], 0.0).then_inc(numbers, 1)
            for i in range(PER_WORD):
                pool.memset(place[:, :, i], float(1 << (DIGIT * i))).then_inc(numbers, 1)
            pool.memset(sign_b[:, 0:MAXB - 2:2], 1.0).then_inc(numbers, 1)
            pool.memset(sign_b[:, 1:MAXB - 2:2], -1.0).then_inc(numbers, 1)

            for n in range(NT):
                cols = slice(n * P, (n + 1) * P)
                pool.wait_ge(xnT_ready, n + 1)
                pool.tensor_tensor(xnT[:, :, cols], xnTh[:, :, cols].bitcast(F32), xnTl[:, :, cols].bitcast(F32),
                                   ALU.add).then_inc(xnT_whole, 1)

            def split_low(e, p, j):
                high_wait(pool, e, j)
                pool.tensor_tensor(piece(WL[p], j), raw(j), piece(WH[p], j).bitcast(F32),
                                   ALU.subtract).then_inc(low_pool, 1)

            for j in LOW_POOL:
                split_low(0, 0, j)
            pool.wait_ge(slots_ready, 1)
            pool.wait_ge(rows_filled, 16 * len(FILLS))
            for n in range(NT):
                r = LAST if n == NT - 1 else P
                for k in range(TOPK):
                    pool.indirect_dma_start(
                        out=xs[:, :], out_offset=bass.IndirectOffsetOnAxis(ap=slot_i[0:r, k, n:n + 1], axis=0),
                        in_=xn[0:r, n, :], in_offset=None).then_inc(rows_moved, 16)

            for j in LOW_POOL:
                split_low(1, 1, j)
            tile_no = pool.alloc_register("pool_tile")
            pool.reg_mov(tile_no, NT + 1)
            pool.wait_ge(y_stored, 16 * (NSH + 1))
            added = pool.alloc_register("rows_added")
            pool.reg_mov(added, 16 * SCATTERS)

            def add_rows(size):
                for t in range(size):
                    pool.wait_ge(y_taken, pool.snap(tile_no, min_val=NT + 1, max_val=NT + MAX_ROUTED))
                    pool.reg_add(tile_no, tile_no, 1)
                    pool.wait_ge(rows_moved, added)
                    pool.reg_add(added, added, 16)
                    pool.indirect_dma_start(
                        out=sums[:, :], out_offset=bass.IndirectOffsetOnAxis(ap=dest[:, t:t + 1], axis=0),
                        in_=ysb[:, t, :], in_offset=None, compute_op=ALU.add).then_inc(rows_moved, 16)

            def expert(e, p):
                if p is not None:
                    for j in LOW_POOL:
                        split_low(e + 1, p, j)
                kind_now = first_kind(pool, regs)
                go_on(pool, regs)
                with pool.If(kind_now > 0):
                    add_rows(WIDE)
                with pool.Else():
                    add_rows(2)
                more = blocks_more(pool, regs)
                with pool.If(more > 0):
                    with pool.Fori(0, more):
                        add_rows(2)
                with pool.Else():
                    pass

            regs = load_words(pool, "pool")
            with pool.Fori(0, (NE - 2) // 2) as q:
                expert(q * 2 + 1, 0)
                expert(q * 2 + 2, 1)
            expert(NEXP - 2, 0)
            expert(NEXP - 1, None)

        @block.scalar
        def _(act):
            act.wait_ge(var_ready, 1)
            act.activation(rstd[:, :], rstd[:, :], ACT.Sqrt).then_inc(std_ready, 1)
            act.wait_ge(par_in, 16 * 6)
            act.activation(cwh[:, :, :], cw[:, :, :], ACT.Copy).then_inc(cwh_ready, 1)
            for n in range(NT):
                act.wait_ge(xnT_psum, n + 1)
                act.activation(xnTh[:, :, n * P:(n + 1) * P],
                               ps[n % 4][:, 0:KD * P].rearrange("p (k t) -> p k t", k=KD),
                               ACT.Copy).then_inc(xnTh_ready, 1)
            def take_srow(b):
                c, w = b * 512, min(512, NPAD - b * 512)
                act.wait_ge(srow_psum, cdiv(c + w, P))
                act.activation(srow[:, c:c + w], ps[b][:, 0:w], ACT.Copy).then_inc(srow_ready, 1)

            for n in range(NT):
                act.wait_ge(node_psum, n + 1)
                act.activation(node[:, n, 0:D], ps[3 + n % 2][:, 0:D], ACT.Copy)
                act.activation(node_adj[:, n, 0:D], ps[3 + n % 2][:, D:2 * D], ACT.Copy).then_inc(node_act, 1)
                if n >= 5 and n % 4 == 1:
                    take_srow(n // 4 - 1)
            take_srow(2)
            act.wait_ge(srow_ready, 3)
            act.wait_ge(node_dve, NT)

            def score(n):
                act.activation(e_sb[:, n, :], srow[:, :], ACT.Identity, bias=scol[:, n, 3:4]).then_inc(score_v, 1)

            score(0)
            for n in range(NT):
                if n + 1 < NT:
                    score(n + 1)
                act.wait_ge(score_w, n + 1)
                act.activation(e_sb[:, n, :], e_sb[:, n, :], ACT.Exp, scale=-1.0).then_inc(score_e, 1)
                act.wait_ge(xb_psum, n + 1)
                act.activation(xb[:, n, :], ps[3 + n % 2][:, 0:D + 2], ACT.Copy).then_inc(xb_ready, 1)
            def split_high(e, p, j):
                stage_wait(act, e, j)
                act.activation(piece(WH[p], j), raw(j), ACT.Copy).then_inc(high_act, 1)

            def take_xT(g, half):
                act.wait_ge(xT_psum, g * 2 + (half + 1))
                if half == 0:
                    act.activation(xTf[:, :, 0:2 * P], ps[X_BANK][:, :].rearrange("p (k t) -> p k t", k=KD),
                                   ACT.Copy).then_inc(xTf_ready, 1)
                else:
                    act.activation(xTf[:, :, 2 * P:BLOCK], ps[X_BANK][:, 0:KD * P].rearrange("p (k t) -> p k t", k=KD),
                                   ACT.Copy).then_inc(xTf_ready, 1)

            def high_xT(k):
                act.activation(xTh[:, k, :], xTf[:, k, :], ACT.Copy).then_inc(xTh_ready, 1)

            act.wait_ge(att_sum, 1)
            act.activation(att[:, :, :], att[:, :, :], ACT.Sigmoid).then_inc(att_ready, 1)
            for n in range(NT):
                if n == NT - 1:
                    take_xT(0, 0)
                    take_xT(0, 1)
                    act.wait_ge(xTf_ready, 2)
                    for k in range(KD):
                        high_xT(k)
                act.wait_ge(z_ready, n + 1)
                act.activation(z[:, n % 2, :], z[:, n % 2, :], ACT.Sigmoid).then_inc(gn_ready, 1)
                if n % 2:
                    split_high(0, 0, n)
                if n in GROUP_ENDS:
                    q = GROUP_ENDS.index(n)
                    part = slice(*GROUPS[q])
                    act.wait_ge(var_ready, 2 + q)
                    act.activation(rstd[:, part], rstd[:, part], ACT.Sqrt).then_inc(std_ready, 1)

            def load_rows(t):
                act.dma_start(xg[:, :, :], xs[bass.ds((t - NT) * P, BLOCK), :].rearrange("(q p) d -> p q d", p=P))\
                    .then_inc(x_loaded, 16)

            def store_own(g):
                act.wait_ge(y_taken, sum(SHARED[:g + 1]))
                first_row, size = sum(SHARED[:g]) * P, SHARED[g]
                act.dma_start(sums[first_row:first_row + size * P, :].rearrange("(q p) d -> p q d", p=P),
                              ysb[:, 0:size, :]).then_inc(y_stored, 16)

            def compute(g, t, size, prep, first=False, rows_next=True, regs=None, n=None):
                n = n or size * P

                def high(c):
                    act.wait_ge(h_done, g * NC + (c + 1))
                    if c >= 2:
                        act.wait_ge(down_done, g * NC + (c - 1))
                    elif not first:
                        act.wait_ge(down_done, g * NC)
                    r = CHUNKS[c]
                    act.activation(hh[0:r, c % 2, 0:n], hid[0:r, c % 2, 0:n], ACT.Copy).then_inc(hh_ready, 1)

                for c in range(NC):
                    if c == 2 and isinstance(g, int) and g:
                        store_own(g - 1)
                    if c:
                        high(c - 1)
                    act.wait_ge(gate_done, g * NC + (c + 1))
                    if c >= 2:
                        act.wait_ge(hl_ready, g * NC + (c - 1))
                    elif not first:
                        act.wait_ge(hl_ready, g * NC)
                    r = CHUNKS[c]
                    act.activation(hid[0:r, c % 2, 0:n], ps[A_BANK[c % 2]][0:r, 0:n], ACT.Silu).then_inc(silu_done, 1)
                    if c == 1 and rows_next:
                        act.wait_ge(xT_psum, g * 2 + 2)
                        if not isinstance(g, int):
                            act.wait_ge(meta_read, g + (1 - NSH))
                        load_rows(t + size)
                    if c == 3 and regs is not None:
                        go_on(act, regs)
                    elif c == 3 and isinstance(g, int) and g == NSH - 2:
                        act.wait_ge(counts_ready, 1)
                        regs_read.append(load_words(act, "act"))
                    for j in pieces_at(c, prep):
                        if j % 2:
                            split_high(prep[0], prep[1], j)
                    take_x = TAKE_X_FIRST if first else TAKE_X
                    if first and c == 4:
                        act.wait_ge(gshift, 1)
                        act.activation(top[:, :, 0:TOPK], top[:, :, 0:TOPK], ACT.Exp).then_inc(gexp_ready, 1)
                    if c == take_x[0]:
                        act.wait_ge(xT_ready, g * KD + KD)
                        take_xT(g + 1, 0)
                    if c == take_x[1]:
                        take_xT(g + 1, 1)
                act.wait_ge(up_done, g * NC + NC)
                act.wait_ge(xTf_ready, g * 2 + 4)
                high_xT(0)
                high(NC - 1)
                for k in range(1, KD):
                    high_xT(k)

            regs_read = []
            for g, size in enumerate(SHARED):
                if g == NSH - 1:
                    act.wait_ge(rows_moved, 16 * SCATTERS)
                compute(g, NT - size, size, (1, 1) if g == NSH - 2 else None, first=g == 0,
                        rows_next=g == NSH - 1)
            store_own(NSH - 1)
            regs, = regs_read
            block_no, tile_no = act.alloc_register("act_block"), act.alloc_register("act_tile")
            act.reg_mov(block_no, NSH)
            act.reg_mov(tile_no, NT)

            def routed(size, prep, regs=None, n=None):
                compute(act.snap(block_no, min_val=NSH, max_val=NSH + MAX_ROUTED // 2),
                        act.snap(tile_no, min_val=NT, max_val=NT + MAX_ROUTED - size), size, prep, regs=regs, n=n)
                act.reg_add(block_no, block_no, 1)
                act.reg_add(tile_no, tile_no, size)

            def expert(e, nxt):
                kind_now = first_kind(act, regs)
                with act.If(kind_now > 0):
                    with act.If(kind_now > 1):
                        routed(WIDE, nxt, regs, NARROW)
                    with act.Else():
                        routed(WIDE, nxt, regs)
                with act.Else():
                    routed(2, nxt, regs)
                more = blocks_more(act, regs)
                with act.If(more > 0):
                    with act.Fori(0, more):
                        routed(2, None)
                with act.Else():
                    pass

            with act.Fori(0, (NE - 2) // 2) as q:
                expert(q * 2 + 1, (q * 2 + 2, 0))
                expert(q * 2 + 2, (q * 2 + 3, 1))
            expert(NEXP - 2, (NEXP - 1, 0))
            expert(NEXP - 1, None)

        @block.vector
        def _(dve):
            steps = [0]

            def link(ins):
                steps[0] += 1
                ins.then_inc(dve_step, 1)
                dve.wait_ge(dve_step, steps[0])

            for i, (a, b) in enumerate(X_PARTS):
                dve.wait_ge(x_in[i], 16)
                for n in range(a, b):
                    last = dve.bn_stats(stats[:, n, :], xres[:, n, :])
            link(last)
            for n in range(NT):
                last = dve.bn_aggr(mv[:, n, :], stats[:, n, :])
            link(last)
            dve.tensor_scalar(rstd[:, :], mv[:, :, 1], EPS, None, ALU.add).then_inc(var_ready, 1)
            dve.wait_ge(std_ready, 1)
            link(dve.reciprocal(rstd[:, :], rstd[:, :]))
            for n in range(NT):
                dve.tensor_scalar(xn[:, n, 0:D], xres[:, n, :], mv[:, n, 0:1], rstd[:, n:n + 1],
                                  ALU.subtract, ALU.mult).then_inc(xn1_ready, 1)
            dve.memset(node[:, :, D:D + 1], 1.0)
            for n in range(NT):
                dve.wait_ge(xnTh_ready, n + 1)
                cols = slice(n * P, (n + 1) * P)
                dve.tensor_tensor(xnTl[:, :, cols], ps[n % 4][:, 0:KD * P].rearrange("p (k t) -> p k t", k=KD),
                                  xnTh[:, :, cols].bitcast(F32), ALU.subtract).then_inc(xnT_ready, 1)
                if n == 3:
                    dve.wait_ge(cwh_ready, 1)
                    dve.tensor_tensor(cwl[:, :, :], cw[:, :, :], cwh[:, :, :].bitcast(F32), ALU.subtract).then_inc(cw_ready, 1)
                if n == 5:
                    dve.wait_ge(u_psum, 1)
                    dve.tensor_copy(cv[:, :, 4:6], ps[7][:, 0:2 * KD].rearrange("p (k c) -> p k c", k=KD)).then_inc(u_ready, 1)
            for n in range(NT):
                dve.wait_ge(node_psum, n + 1)
                dve.tensor_copy(node_adj[:, n, D:D + 2], ps[5 + n % 2][:, 0:2])
                dve.tensor_copy(scol[:, n, :], ps[5 + n % 2][:, 2:6]).then_inc(node_dve, 1)
                dve.wait_ge(node_dve, n + 1)
                if n >= 2:
                    dve.wait_ge(srow_psum, n - 1)
                dve.tensor_copy(srep[:, n % 2, :], scol[:, n, 2:3].to_broadcast([P, P])).then_inc(srep_ready, 1)
            dve.wait_ge(adj_in, 16)

            def mask(n):
                dve.wait_ge(score_e, n + 1)
                dve.scalar_tensor_tensor(out=e_sb[:, n, :], in0=adj_sb[:, n, :], scalar=0.0, in1=e_sb[:, n, :],
                                         op0=ALU.not_equal, op1=ALU.mult).then_inc(e_ready, 1)

            for n in range(NT):
                dve.wait_ge(score_v, n + 1)
                dve.scalar_tensor_tensor(out=e_sb[:, n, :], in0=e_sb[:, n, :], scalar=0.01, in1=e_sb[:, n, :],
                                         op0=ALU.mult, op1=ALU.max).then_inc(score_w, 1)
                if n:
                    mask(n - 1)
            mask(NT - 1)
            dve.wait_ge(xb_ready, NT)
            dve.sem_inc(adj_free, 1)
            dve.wait_ge(late_in, 48)
            link(dve.tensor_tensor(att[:, :, :], xb[:, :, D:D + 2], scol[:, :, 0:2], ALU.add))
            dve.tensor_tensor(att[:, :, :], att[:, :, :], abias[:, :].unsqueeze(1).to_broadcast([P, NT, 2]),
                              ALU.add).then_inc(att_sum, 1)
            link(dve.tensor_tensor(xb[:, :, 0:D], xb[:, :, 0:D], gbias[:, :].unsqueeze(1).to_broadcast([P, NT, D]),
                                   ALU.add))
            dve.wait_ge(att_ready, 1)
            link(dve.tensor_tensor(xb[:, :, 0:D], xb[:, :, 0:D], att[:, :, 1:2].to_broadcast([P, NT, D]), ALU.mult))

            def mix(n):
                pa = ps[n % 3]
                dve.wait_ge(xa_psum, n + 1)
                link(dve.tensor_scalar(small[:, n, 0:1], pa[:, D:D + 1], ATTN_EPS, None, ALU.add))
                link(dve.reciprocal(small[:, n, 1:2], small[:, n, 0:1]))
                link(dve.tensor_tensor(small[:, n, 2:3], small[:, n, 1:2], att[:, n, 0:1], ALU.mult))
                dve.scalar_tensor_tensor(out=z[:, n % 2, :], in0=pa[:, 0:D], scalar=small[:, n, 2:3],
                                         in1=xb[:, n, 0:D], op0=ALU.mult, op1=ALU.add).then_inc(z_ready, 1)

            def add_graph(n):
                dve.wait_ge(gn_ready, n + 1)
                link(dve.tensor_tensor(xres[:, n, :], xres[:, n, :], z[:, n % 2, :], ALU.add))
                link(dve.bn_stats(stats[:, n, :], xres[:, n, :]))
                link(dve.bn_aggr(mv[:, n, :], stats[:, n, :]))
                last = dve.tensor_scalar(rstd[:, n:n + 1], mv[:, n, 1:2], EPS, None, ALU.add)
                if n in GROUP_ENDS:
                    last.then_inc(var_ready, 1)

            def norm(n):
                firsts = [a for a, _ in GROUPS]
                if n in firsts:
                    q = firsts.index(n)
                    dve.wait_ge(std_ready, 2 + q)
                    part = slice(*GROUPS[q])
                    link(dve.reciprocal(rstd[:, part], rstd[:, part]))
                dve.tensor_scalar(xn[:, n, 0:D], xres[:, n, :], mv[:, n, 0:1], rstd[:, n:n + 1],
                                  ALU.subtract, ALU.mult).then_inc(xn2_ready, 1)

            def take_xT2(n):
                bank, o, count = norm_bank(n)
                dve.wait_ge(xT2_psum, count)
                dve.tensor_copy(xT2[:, n % 3, :, :], ps[bank][:, o:o + KD * P].rearrange("p (k t) -> p k t", k=KD))\
                    .then_inc(xT2_ready, 1)

            def route(n):
                bank, o, count = gate_bank(n)
                dve.wait_ge(gate_psum, count)
                dve.tensor_tensor(gates[:, n, :], ps[bank][:, o:o + NE], rbias[:, :], ALU.add).then_inc(gate_read, 1)
                dve.wait_ge(gate_read, n + 1)
                link(dve.max(top[:, n, :], gates[:, n, :]))
                link(dve.max_index(top_i[:, n, :], top[:, n, :], gates[:, n, :]))

            def low_xT(g, k):
                dve.wait_ge(xTh_ready, g * KD + (k + 1))
                dve.tensor_tensor(xTl[:, k, :], xTf[:, k, :], xTh[:, k, :].bitcast(F32), ALU.subtract)\
                    .then_inc(xT_ready, 1)

            def split(e, p, j):
                if j % 2 == 0:
                    stage_wait(dve, e, j)
                    dve.tensor_copy(piece(WH[p], j), raw(j)).then_inc(high_dve, 1)
                if j % 4 == 0:
                    high_wait(dve, e, j)
                    dve.tensor_tensor(piece(WL[p], j), raw(j), piece(WH[p], j).bitcast(F32), ALU.subtract)\
                        .then_inc(low_dve, 1)

            for i in range(NT - 1):
                mix(i)
                if i:
                    add_graph(i - 1)
                for t in ROUTE.get(i, ()):
                    norm(t)
                for t in ROUTE.get(i - 1, ()):
                    take_xT2(t)
                for t in ROUTE.get(i - 2, ()):
                    route(t)
                if i:
                    split(0, 0, i - 1)
            mix(NT - 1)
            for t in ROUTE[NT - 2]:
                take_xT2(t)
            for k in range(KD):
                low_xT(0, k)
            add_graph(NT - 2)
            add_graph(NT - 1)
            for t in ROUTE[NT - 3]:
                route(t)
            for j in range(NT - 2, NC):
                split(0, 0, j)
            for t in MID:
                norm(t)
            for t in ROUTE[NT - 2]:
                route(t)
            for t in MID:
                take_xT2(t)

            def norm_late():
                for n in LATE:
                    norm(n)

            def take_late():
                for n in MID:
                    route(n)
                for n in LATE:
                    take_xT2(n)

            def choose():
                for n in LATE:
                    route(n)
                dve.wait_ge(numbers, 9 + PER_WORD)
                dve.wait_ge(masks, 3)
                link(dve.tensor_copy(top_f[:, :, :], top_i[:, :, 0:TOPK]))
                for k in range(TOPK):
                    last = dve.tensor_tensor(onehot[:, k, :, :], number_e[:, :].unsqueeze(1).to_broadcast([P, NT, NE]),
                                             top_f[:, :, k:k + 1].to_broadcast([P, NT, NE]), ALU.is_equal)
                link(last)
                link(dve.tensor_scalar(onehot[:, :, NT - 1, :], onehot[:, :, NT - 1, :], valid[:, 0:1], None, ALU.mult))
                link(dve.tensor_tensor(pick[:, 0:2, :, :], onehot[:, 0:2, :, :], onehot[:, 2:4, :, :], ALU.add))
                dve.tensor_tensor(chosen[:, :, :], pick[:, 0, :, :], pick[:, 1, :, :], ALU.add).then_inc(chosen_ready, 1)
                dve.tensor_tensor(top_f[:, :, :], top[:, :, 0:TOPK], top[:, :, 0:1].to_broadcast([P, NT, TOPK]),
                                  ALU.subtract).then_inc(gate_read, 1)
                dve.wait_ge(gate_read, NT + 1)
                dve.tensor_copy(top[:, :, 0:TOPK], top_f[:, :, :]).then_inc(gshift, 1)

            def count_tiles():
                dve.wait_ge(pos_psum, 1)
                each = ps[X_BANK][:, NT * NE:2 * NT * NE].rearrange("p (n e) -> p n e", n=NT)
                for n in range(NT):
                    link(dve.tensor_tensor(base[:, n + 1, :], base[:, n, :], each[:, n, :], ALU.add))
                earlier = ps[X_BANK][:, 0:NT * NE].rearrange("p (n e) -> p n e", n=NT)
                dve.tensor_tensor(slot[:, :, :], earlier, base[:, 0:NT, :], ALU.add).then_inc(pos_read, 1)
                dve.wait_ge(pos_read, 1)

            def count_blocks():
                link(dve.tensor_tensor(above[:, :, :], base[:, NT, :].unsqueeze(2).to_broadcast([P, NE, MAXB - 2]),
                                       number_b[:, :].unsqueeze(1).to_broadcast([P, NE, MAXB - 2]), ALU.is_gt))
                link(dve.tensor_reduce(slot0[:, :], above[:, :, :], AX.X, ALU.add))
                link(dve.tensor_scalar(ntile[:, :], slot0[:, :], 2.0, None, ALU.add))
                link(dve.tensor_tensor(above[:, :, :], above[:, :, :],
                                       sign_b[:, :].unsqueeze(1).to_broadcast([P, NE, MAXB - 2]), ALU.mult))
                link(dve.tensor_reduce(odd[:, :], above[:, :, :], AX.X, ALU.add))
                link(dve.tensor_tensor(extra[:, :], ntile[:, :], odd[:, :], ALU.subtract))
                link(dve.tensor_scalar(extra[:, :], extra[:, :], 0.5, -1.0, ALU.mult, ALU.add))
                link(dve.tensor_scalar(rest[:, :], ntile[:, :], -float(P), float(P), ALU.mult, ALU.add))
                link(dve.tensor_tensor(rest[:, :], rest[:, :], base[:, NT, :], ALU.add))
                link(dve.scalar_tensor_tensor(out=kind[:, :], in0=rest[:, :], scalar=P / 2, in1=odd[:, :],
                                              op0=ALU.is_le, op1=ALU.mult))
                link(dve.tensor_tensor(kind[:, :], kind[:, :], odd[:, :], ALU.add))
                dve.tensor_scalar(upto[:, :], rest[:, :], float(2 * P), None, ALU.add)
                link(dve.tensor_scalar(gap[:, :], rest[:, :], -1.0, float(P), ALU.mult, ALU.add))
                link(dve.tensor_tensor(gap[:, :], gap[:, :], odd[:, :], ALU.mult))
                link(dve.tensor_tensor_scan(tiles_to[:, :], ones_e[:, :], ntile[:, :], 0.0, ALU.mult, ALU.add))
                link(dve.tensor_scalar(total_f[:, :], tiles_to[:, NE - 1:NE], float(NT), None, ALU.add))
                digits = digit[:, :, :].rearrange("p w i -> p (w i)")[:, 0:NE]
                link(dve.scalar_tensor_tensor(out=digits, in0=extra[:, :], scalar=4.0, in1=kind[:, :],
                                              op0=ALU.mult, op1=ALU.add))
                link(dve.tensor_tensor(digit[:, :, :], digit[:, :, :], place[:, :, :], ALU.mult))
                link(dve.tensor_reduce(words[:, :], digit[:, :, :], AX.X, ALU.add))
                dve.tensor_copy(words_i[:, :], words[0:1, :])
                dve.tensor_copy(total_i[:, :], total_f[0:1, :]).then_inc(counts_ready, 1)

            def find_slots():
                past = pick[:, 0, :, :]
                link(dve.tensor_tensor(past, slot[:, :, :], upto[:, :].unsqueeze(1).to_broadcast([P, NT, NE]), ALU.is_ge))
                link(dve.tensor_tensor(past, past, gap[:, :].unsqueeze(1).to_broadcast([P, NT, NE]), ALU.mult))
                link(dve.tensor_tensor(slot[:, :, :], slot[:, :, :], past, ALU.add))
                link(dve.tensor_tensor(slot0[:, :], tiles_to[:, :], ntile[:, :], ALU.subtract))
                link(dve.tensor_scalar(slot0[:, :], slot0[:, :], float(P), None, ALU.mult))
                link(dve.tensor_tensor(slot[:, :, :], slot[:, :, :], slot0[:, :].unsqueeze(1).to_broadcast([P, NT, NE]),
                                       ALU.add))
                link(dve.tensor_tensor(pick[:, :, :, :], onehot[:, :, :, :],
                                       slot[:, :, :].unsqueeze(1).to_broadcast([P, TOPK, NT, NE]), ALU.mult))
                link(dve.tensor_reduce(slot_k[:, :, :], pick[:, :, :, :], AX.X, ALU.add))
                link(dve.tensor_copy(slot_i[:, :, :], slot_k[:, :, :]))

            def weigh():
                dve.wait_ge(gexp_ready, 1)
                link(dve.tensor_reduce(gsum[:, :], top[:, :, 0:TOPK], AX.X, ALU.add))
                link(dve.reciprocal(gsum[:, :], gsum[:, :]))
                link(dve.tensor_tensor(top_f[:, :, :], top[:, :, 0:TOPK],
                                       gsum[:, :].unsqueeze(2).to_broadcast([P, NT, TOPK]), ALU.mult))
                for k in range(TOPK):
                    last = dve.tensor_tensor(pick[:, k, :, :], onehot[:, k, :, :],
                                             top_f[:, :, k:k + 1].to_broadcast([P, NT, NE]), ALU.mult)
                link(last)
                link(dve.tensor_tensor(pick[:, 0:2, :, :], pick[:, 0:2, :, :], pick[:, 2:4, :, :], ALU.add))
                dve.tensor_tensor(xn[:, :, D + 1:PW], pick[:, 0, :, :], pick[:, 1, :, :], ALU.add).then_inc(slots_ready, 1)

            ROUTING = {0: norm_late, 1: take_late, 2: choose, 4: count_tiles, 5: count_blocks, 6: find_slots, 7: weigh}

            def compute(g, t, size, e, prep, regs=None, n=None):
                n = n or size * P
                if e is not None:
                    dve.tensor_copy(meta[:, :, :], xg[:, :, D:PW]).then_inc(meta_read, 1)

                def low(c):
                    r = CHUNKS[c]
                    dve.wait_ge(hh_ready, g * NC + (c + 1))
                    dve.tensor_tensor(hl[0:r, c % 2, 0:n], hid[0:r, c % 2, 0:n], hh[0:r, c % 2, 0:n].bitcast(F32),
                                      ALU.subtract).then_inc(hl_ready, 1)

                for c in range(NC):
                    if c:
                        low(c - 1)
                    r = CHUNKS[c]
                    dve.wait_ge(up_done, g * NC + (c + 1))
                    dve.wait_ge(silu_done, g * NC + (c + 1))
                    dve.tensor_tensor(hid[0:r, c % 2, 0:n], hid[0:r, c % 2, 0:n], ps[B_BANK[c % 2]][0:r, 0:n], ALU.mult)\
                        .then_inc(h_done, 1)
                    if c == 3 and regs is not None:
                        go_on(dve, regs)
                    elif c == 3 and isinstance(g, int) and g == NSH - 2:
                        dve.wait_ge(counts_ready, 1)
                        regs_read.append(load_words(dve, "dve"))
                    for j in pieces_at(c, prep):
                        split(prep[0], prep[1], j)
                    if isinstance(g, int) and g == 0 and c in ROUTING:
                        ROUTING[c]()
                    if e is not None and c == 4:
                        dve.wait_ge(y_stored, 16 * (NSH + 1))
                        dve.wait_ge(meta_read, g + (1 - NSH))
                        dve.wait_ge(rows_moved, t * 16 + 16 * (SCATTERS - NT))
                        dve.tensor_copy(dest[:, :], meta[:, :, 0])
                        dve.tensor_copy(wcol[:, :], meta[:, :, bass.ds(e, 1)].rearrange("p q a -> p (q a)"))\
                            .then_inc(meta_ready, 1)
                low(NC - 1)
                for k in range(KD):
                    low_xT(g + 1, k)
                dve.wait_ge(down_done, g * NC + NC)
                if e is None:
                    dve.wait_ge(y_stored, g * 16 + 16)
                    for q in range(size):
                        dve.tensor_tensor(ysb[:, q, :], ps[Y_BANK[q]][:, 0:D], xres[:, t + q, :], ALU.add)\
                            .then_inc(y_taken, 1)
                else:
                    dve.wait_ge(meta_ready, g + (1 - NSH))
                    for q in range(size):
                        m = min(P, n - q * P)
                        dve.tensor_scalar(ysb[0:m, q, :], ps[Y_BANK[q]][0:m, 0:D], wcol[0:m, q:q + 1], None, ALU.mult)\
                            .then_inc(y_taken, 1)

            regs_read = []
            for g, size in enumerate(SHARED):
                compute(g, sum(SHARED[:g]), size, None, (1, 1) if g == NSH - 2 else None)
            regs, = regs_read
            block_no, tile_no = dve.alloc_register("dve_block"), dve.alloc_register("dve_tile")
            dve.reg_mov(block_no, NSH)
            dve.reg_mov(tile_no, NT)

            def routed(size, e, prep, regs=None, n=None):
                compute(dve.snap(block_no, min_val=NSH, max_val=NSH + MAX_ROUTED // 2),
                        dve.snap(tile_no, min_val=NT, max_val=NT + MAX_ROUTED - size), size, e, prep, regs=regs, n=n)
                dve.reg_add(block_no, block_no, 1)
                dve.reg_add(tile_no, tile_no, size)

            def expert(e, nxt):
                kind_now = first_kind(dve, regs)
                with dve.If(kind_now > 0):
                    with dve.If(kind_now > 1):
                        routed(WIDE, e, nxt, regs, NARROW)
                    with dve.Else():
                        routed(WIDE, e, nxt, regs)
                with dve.Else():
                    routed(2, e, nxt, regs)
                more = blocks_more(dve, regs)
                with dve.If(more > 0):
                    with dve.Fori(0, more):
                        routed(2, e, None)
                with dve.Else():
                    pass

            with dve.Fori(0, (NE - 2) // 2) as q:
                expert(q * 2 + 1, (q * 2 + 2, 0))
                expert(q * 2 + 2, (q * 2 + 3, 1))
            expert(NEXP - 2, (NEXP - 1, 0))
            expert(NEXP - 1, None)

        @block.tensor
        def _(pe):
            pe.wait_ge(masks, 1)
            def w_columns():
                pe.wait_ge(par_in, 16 * 6)
                for c in range(KD):
                    for k in range(KD):
                        last = pe.matmul(ps[7][:, 2 * c:2 * c + 2], wsT[:, k, c * P:(c + 1) * P], ac[:, k, :],
                                         start=(k == 0), stop=(k == KD - 1))
                last.then_inc(u_psum, 1)

            def transpose_xn(n):
                pe.wait_ge(xn1_ready, n + 1)
                if n >= 4:
                    pe.wait_ge(xnT_ready, n - 3)
                for k in range(KD):
                    last = pe.transpose(ps[n % 4][:, k * P:(k + 1) * P], xn[:, n, k * P:(k + 1) * P], ident[:, :])
                last.then_inc(xnT_psum, 1)

            def node_row(n):
                cols = slice(n * P, (n + 1) * P)
                pe.wait_ge(xnT_ready, max(n + 1, (NT - 1 - 3) // 4 * 4 + 3 + 1))
                if n >= 2:
                    pe.wait_ge(node_act, n - 1)
                    pe.wait_ge(node_dve, n - 1)
                for k in range(KD):
                    for m, (a, w) in enumerate(((xnTh, cwh), (xnTl, cwh), (xnTh, cwl))):
                        pe.matmul(ps[3 + n % 2][:, :], a[:, k, cols], w[:, k, :],
                                  start=(k == 0 and m == 0), stop=(k == KD - 1 and m == 2))
                pe.wait_ge(u_ready, 1)
                pe.wait_ge(xnT_whole, n + 1)
                for k in range(KD):
                    last = pe.matmul(ps[5 + n % 2][:, 0:6], xnT[:, k, cols], cv[:, k, :],
                                     start=(k == 0), stop=(k == KD - 1))
                last.then_inc(node_psum, 1)

            def left_row(n):
                pe.wait_ge(srep_ready, n + 1)
                pe.matmul(ps[n // 4][:, n % 4 * P:(n % 4 + 1) * P], srep[:, n % 2, :], ident[:, :],
                          start=True, stop=True).then_inc(srow_psum, 1)

            for n in range(NT):
                transpose_xn(n)
                if n == 3:
                    w_columns()
            pe.wait_ge(cw_ready, 1)
            for n in range(NT):
                node_row(n)
                if n:
                    left_row(n - 1)
            left_row(NT - 1)
            pe.wait_ge(adj_in, 16)
            pe.wait_ge(node_act, NT)
            pe.wait_ge(node_dve, NT)
            for i in range(NT):
                if i >= 2:
                    pe.wait_ge(xb_ready, i - 1)
                for n in range(NT):
                    last = pe.matmul(ps[3 + i % 2][:, 0:D + 2], adj_sb[:, n, i * P:(i + 1) * P], node_adj[:, n, :],
                                     start=(n == 0), stop=(n == NT - 1))
                last.then_inc(xb_psum, 1)
            def gate(t):
                pe.wait_ge(xT2_ready, t + 1)
                if 2 <= t < ROUTE[NT - 2][0]:
                    pe.wait_ge(gate_read, t - 1)
                bank, o, _ = gate_bank(t)
                for k in range(KD):
                    last = pe.matmul(ps[bank][:, o:o + NE], xT2[:, t % 3, k, :], gatew[:, k, :],
                                     start=(k == 0), stop=(k == KD - 1))
                last.then_inc(gate_psum, 1)

            def transpose_norm(t):
                pe.wait_ge(xn2_ready, t + 1)
                if t < MID[0] and t >= 2:
                    pe.wait_ge(xT2_ready, t - 1)
                bank, o, _ = norm_bank(t)
                for k in range(KD):
                    last = pe.transpose(ps[bank][:, o + k * P:o + (k + 1) * P], xn[:, t, k * P:(k + 1) * P], ident[:, :])
                last.then_inc(xT2_psum, 1)

            def transpose_x(half, rows):
                tiles = (0, 1) if half == 0 else (2,)
                for q in tiles:
                    for k in range(KD):
                        o = (k * len(tiles) + q % 2) * P if half == 0 else k * P
                        last = pe.transpose(ps[X_BANK][:, o:o + P], rows(q)[:, k * P:(k + 1) * P], ident[:, :])
                last.then_inc(xT_psum, 1)

            def own_rows(g):
                first = sum(SHARED[:g])
                return lambda q: xn[:, min(first + q, NT - 1), :]

            def scattered_rows(q):
                return xg[:, q, :]

            for i in range(NT):
                if i == 0:
                    pe.wait_ge(srow_ready, 3)
                if i >= 3:
                    pe.wait_ge(z_ready, i - 2)
                for n in range(NT):
                    if i == 0:
                        pe.wait_ge(e_ready, n + 1)
                    last = pe.matmul(ps[i % 3][:, 0:D + 1], e_sb[:, n, i * P:(i + 1) * P], node[:, n, :],
                                     start=(n == 0), stop=(n == NT - 1))
                last.then_inc(xa_psum, 1)
                if i == NT - 1:
                    transpose_x(0, own_rows(0))
                for t in ROUTE.get(i - 2, ()):
                    gate(t)
                if i == NT - 1:
                    pe.wait_ge(xTf_ready, 1)
                    transpose_x(1, own_rows(0))
                for t in ROUTE.get(i - 1, ()):
                    if t == 0:
                        pe.wait_ge(xb_ready, NT)
                    transpose_norm(t)

            def up(p, g, c, n):
                r, at = CHUNKS[c], AT[c]
                for m, (bank, done) in enumerate(((A_BANK, gate_done), (B_BANK, up_done))):
                    terms = [(w, x, k) for w, x in ((WH, xTh), (WL, xTh), (WH, xTl)) for k in range(KD)]
                    for s, (w, x, k) in enumerate(terms):
                        if c == 0 and m == 0 and s == 2 * KD:
                            pe.wait_ge(xT_ready, g * KD + KD)
                        o = at + (m * KD + k) * r
                        last = pe.matmul(ps[bank[c % 2]][0:r, 0:n], w[p][:, o:o + r], x[:, k, 0:n],
                                         start=(s == 0), stop=(s == len(terms) - 1))
                    last.then_inc(done, 1)

            def down(p, g, c, size, n):
                r, o = CHUNKS[c], AT[c] + 2 * KD * CHUNKS[c]
                tiles = [(Y_BANK[q], q * P, min((q + 1) * P, n)) for q in range(size)]
                pe.wait_ge(hh_ready, g * NC + (c + 1))
                for y, a, b in tiles:
                    for s, w in enumerate((WL, WH)):
                        pe.matmul(ps[y][0:b - a, 0:D], hh[0:r, c % 2, a:b], w[p][0:r, o:o + D],
                                  start=(c == 0 and s == 0), stop=False)
                pe.wait_ge(hl_ready, g * NC + (c + 1))
                for y, a, b in tiles:
                    last = pe.matmul(ps[y][0:b - a, 0:D], hl[0:r, c % 2, a:b], WH[p][0:r, o:o + D],
                                     start=False, stop=(c == NC - 1))
                last.then_inc(down_done, 1)

            def transpose_mid():
                pe.wait_ge(gate_read, ROUTE[NT - 2][0])
                pe.wait_ge(xT2_ready, MID[0])
                for t in ROUTE[NT - 2]:
                    gate(t)
                for t in MID:
                    transpose_norm(t)

            def middle():
                pe.wait_ge(gate_read, MID[0])
                for t in MID:
                    gate(t)
                pe.wait_ge(xTf_ready, 2)
                for t in LATE:
                    transpose_norm(t)

            def gate_late():
                pe.wait_ge(xT2_ready, NT)
                for t in LATE:
                    gate(t)

            def positions():
                pe.wait_ge(masks, 3)
                pe.wait_ge(chosen_ready, 1)
                pe.wait_ge(gate_read, NT)
                picked = chosen[:, :, :].rearrange("p n e -> p (n e)")
                pe.matmul(ps[X_BANK][:, 0:NT * NE], tri[:, :], picked, start=True, stop=True)
                pe.matmul(ps[X_BANK][:, NT * NE:2 * NT * NE], ones[:, :], picked, start=True, stop=True)\
                    .then_inc(pos_psum, 1)

            ROUTING = {0: transpose_mid, 1: middle, 2: gate_late, 3: positions}

            def compute(g, t, size, p, e, next_rows, loaded, regs=None, n=None):
                n = n or size * P
                first = isinstance(g, int) and g == 0
                take_x = TAKE_X_FIRST if first else TAKE_X
                pe.wait_ge(xTh_ready, g * KD + KD)
                for c in range(NC + LAG):
                    if c < NC:
                        if e is not None:
                            low_wait(pe, e, c)
                        if c == 1 and first:
                            pe.wait_ge(xT2_ready, MID[0])
                        if c >= 2:
                            pe.wait_ge(h_done, g * NC + (c - 1))
                        up(p, g, c, n)
                    if first and c in ROUTING:
                        ROUTING[c]()
                    if c == 3 and regs is not None:
                        go_on(pe, regs)
                    elif c == 3 and isinstance(g, int) and g == NSH - 2:
                        pe.wait_ge(counts_ready, 1)
                        regs_read.append(load_words(pe, "pe"))
                    if c == LAG and first:
                        pe.wait_ge(gate_read, LATE[0])
                    elif c == LAG:
                        pe.wait_ge(y_taken, t)
                    if c >= LAG:
                        down(p, g, c - LAG, size, n)
                    if c == take_x[0]:
                        if loaded:
                            pe.wait_ge(x_loaded, g * 16 + 16 * (2 - NSH))
                        elif g == 0:
                            pe.wait_ge(pos_read, 1)
                        transpose_x(0, next_rows)
                    if c == take_x[1]:
                        pe.wait_ge(xTf_ready, g * 2 + 3)
                        transpose_x(1, next_rows)

            pe.wait_ge(z_ready, NT)
            regs_read = []
            for g, size in enumerate(SHARED):
                last_own = g == NSH - 1
                compute(g, sum(SHARED[:g]), size, 0, 0 if g == 0 else None,
                        scattered_rows if last_own else own_rows(g + 1), last_own)
            regs, = regs_read
            block_no, tile_no = pe.alloc_register("pe_block"), pe.alloc_register("pe_tile")
            pe.reg_mov(block_no, NSH)
            pe.reg_mov(tile_no, NT)

            def routed(size, p, e, regs=None, n=None):
                compute(pe.snap(block_no, min_val=NSH, max_val=NSH + MAX_ROUTED // 2),
                        pe.snap(tile_no, min_val=NT, max_val=NT + MAX_ROUTED - size), size, p, e, scattered_rows, True, regs, n)
                pe.reg_add(block_no, block_no, 1)
                pe.reg_add(tile_no, tile_no, size)

            def expert(e, p):
                kind_now = first_kind(pe, regs)
                with pe.If(kind_now > 0):
                    with pe.If(kind_now > 1):
                        routed(WIDE, p, e, regs, NARROW)
                    with pe.Else():
                        routed(WIDE, p, e, regs)
                with pe.Else():
                    routed(2, p, e, regs)
                more = blocks_more(pe, regs)
                with pe.If(more > 0):
                    with pe.Fori(0, more):
                        routed(2, p, None)
                with pe.Else():
                    pass

            with pe.Fori(0, (NE - 2) // 2) as q:
                expert(q * 2 + 1, 1)
                expert(q * 2 + 2, 0)
            expert(NEXP - 2, 1)
            expert(NEXP - 1, 0)


def _layout(inputs):
    import numpy as np

    a = {k: np.asarray(v) for k, v in inputs.items()}
    n, d = a["x"].shape
    pad = cdiv(n, P) * P
    x = np.zeros((pad, d), a["x"].dtype)
    x[:n] = a["x"]
    adj = np.zeros((pad, pad), a["adj"].dtype)
    adj[:n, :n] = a["adj"].T
    wa, wb, a_sa = a["L0_gnn_Wa"], a["L0_gnn_Wb"], a["L0_gnn_a_sa"]
    w1 = np.concatenate([a["L0_ffn_sw1"][None], a["L0_ffn_w1"]])
    w2 = np.concatenate([a["L0_ffn_sw2"][None], a["L0_ffn_w2"]])
    w3 = np.concatenate([a["L0_ffn_sw3"][None], a["L0_ffn_w3"]])
    ne, _, h = w1.shape
    chunks = hidden_chunks(h)
    total = sum(chunks)

    def wide(w, axis, n):
        widths = [(0, 0)] * 3
        widths[axis] = (0, n - h)
        return np.pad(w, widths)

    ups = [wide(w, 2, total).reshape(ne, d // P, P, total) for w in (w1, w2)]
    down = wide(w3, 1, cdiv(total, P) * P).reshape(ne, len(chunks), P, d)
    parts = []
    for c, r in enumerate(chunks):
        parts += [u[:, k, :, c * P:c * P + r] for u in ups for k in range(d // P)] + [down[:, c]]
    return {
        "x": x,
        "adjT": adj,
        "w_sa": a["L0_gnn_W_sa"],
        "w_saT": a["L0_gnn_W_sa"].T,
        "w_gcn": a["L0_gnn_W_gcnb"],
        "a_cols": a_sa.reshape(2, d).T,
        "attn_cols": np.stack([wa[0, :d], wb[0, :d], wa[0, d:], wb[0, d:]], axis=1),
        "attn_bias": np.concatenate([a["L0_gnn_ba"], a["L0_gnn_bb"]]),
        "gcn_bias": a["L0_gnn_b_gcnb"],
        "gate_w": a["L0_ffn_gate_w"],
        "routing_bias": a["L0_ffn_routing_bias"],
        "w_ffn": np.concatenate(parts, axis=2),
    }


def kernel(**inputs):
    import numpy as np
    import concourse.bacc as bacc
    from concourse.bass_utils import run_bass_kernel_spmd

    shape = np.asarray(inputs["x"]).shape
    nc = bacc.Bacc("TRN2", target_bir_lowering=False, num_devices=1)
    arrays, args = {}, []
    for name, a in _layout(inputs).items():
        arrays[f"in_{name}"] = np.ascontiguousarray(a)
        args.append(nc.dram_tensor(f"in_{name}", a.shape, mybir.dt.from_np(a.dtype), kind="ExternalInput").ap())
    out = nc.dram_tensor("out", shape, F32, kind="ExternalOutput").ap()
    hidden = np.asarray(inputs["L0_ffn_sw1"]).shape[1]
    graph_attention_and_routed_experts(nc, *args, hidden, out)
    r = run_bass_kernel_spmd(nc, [arrays], core_ids=[0])
    return r.results[0]["out"]
```
